# Optimizing a Trainium2 kernel written in Bass

```python
import numpy as np
import jax
import jax.numpy as jnp

def _softmax(x, axis=-1):
    return jax.nn.softmax(x, axis=axis)

def _gelu(x):
    return jax.nn.gelu(x, approximate=True)

def _silu(x):
    return jax.nn.silu(x)

def _sigmoid(x):
    return jax.nn.sigmoid(x)

def _layernorm(x, axis=-1, eps=1e-05):
    m = jnp.mean(x, axis=axis, keepdims=True)
    v = jnp.var(x, axis=axis, keepdims=True)
    return (x - m) / jnp.sqrt(v + eps)

def _scatter_add(tgt, idx, src, axis=0):
    return tgt.at[idx].add(src)

def _segment_sum(src, seg, n):
    return jax.ops.segment_sum(src, seg, n)
kernel_name = 'mk_flamingo_gated_d1_seqx_r8_bcef39'

def setup_inputs(seed: int=0):
    np.random.seed(seed)
    _w = jnp.asarray

    def _rec_inputs():
        import jax
        import jax.numpy as jnp
        _rk = jax.random.key(seed)
        x = 0.0001212 + 1 * jax.random.normal(jax.random.fold_in(_rk, 1), (8, 128, 128), jnp.float32)
        _lenS = 128 - jax.random.randint(jax.random.fold_in(_rk, 7), (8,), 0, max(1, 128 // 4) + 1, jnp.int32)
        _lenS2 = 128 - jax.random.randint(jax.random.fold_in(_rk, 8), (8,), 0, max(1, 128 // 4) + 1, jnp.int32)
        _ctx_1024P = jax.random.normal(jax.random.fold_in(_rk, 11), (8, 16, 128), jnp.float32)
        _ctx_1024c = jax.random.dirichlet(jax.random.fold_in(_rk, 511), 0.3 * jnp.ones((16,), jnp.float32), (8, 128))
        _ctx_1024t = jnp.einsum('bsk,bkd->bsd', _ctx_1024c, _ctx_1024P)
        _ctx_1024t = _ctx_1024t * jax.lax.rsqrt(jnp.mean(jnp.square(_ctx_1024t)) + 1e-12) * 0.953939
        ctx_1024 = -0.000125008 + 0.999885 * (_ctx_1024t + 0.3 * jax.random.normal(jax.random.fold_in(_rk, 611), (8, 128, 128), jnp.float32))
        _g = jax.random.normal(jax.random.fold_in(_rk, 9001), (2, 1), jnp.float32)
        _g = jnp.sign(_g) * jnp.maximum(jnp.abs(_g), 1.0) + (_g == 0) * 1.0
        g_xattn = _g[0]
        g_ffn = _g[1]
        return (x, ctx_1024, g_xattn, g_ffn)
    x, ctx_1024, g_xattn, g_ffn = _rec_inputs()

    def _L0_xattn_setup():
        import jax, jax.numpy as jnp
        import numpy as np
        B, L, D_MODEL, N_HEADS = (4, 1024, 128, 16)
        D_DEPTH = D_MODEL // N_HEADS

        def _split_heads(x):
            b, l, _ = x.shape
            return x.reshape(b, l, N_HEADS, D_DEPTH).transpose(0, 2, 1, 3)

        def _combine_heads(x):
            b, _, l, _ = x.shape
            return x.transpose(0, 2, 1, 3).reshape(b, l, D_MODEL)
        key = jax.random.key(seed)
        ks = jax.random.split(key, 8)
        s = 1.0 / np.sqrt(D_MODEL)
        return {'v': jax.random.normal(ks[0], (B, L, D_MODEL), dtype=jnp.float32), 'k': jax.random.normal(ks[1], (B, L, D_MODEL), dtype=jnp.float32), 'q': jax.random.normal(ks[2], (B, L, D_MODEL), dtype=jnp.float32), 'wq_w': jax.random.normal(ks[3], (D_MODEL, D_MODEL), dtype=jnp.float32) * s, 'wq_b': jnp.zeros((D_MODEL,), jnp.float32), 'wk_w': jax.random.normal(ks[4], (D_MODEL, D_MODEL), dtype=jnp.float32) * s, 'wk_b': jnp.zeros((D_MODEL,), jnp.float32), 'wv_w': jax.random.normal(ks[5], (D_MODEL, D_MODEL), dtype=jnp.float32) * s, 'wv_b': jnp.zeros((D_MODEL,), jnp.float32), 'wc_w': jax.random.normal(ks[6], (D_MODEL, D_MODEL), dtype=jnp.float32) * s, 'wc_b': jnp.zeros((D_MODEL,), jnp.float32)}
    _L0_xattn_all = _L0_xattn_setup()
    _L0_xattn_in = {k: v for k, v in _L0_xattn_all.items() if k in ('wq_w', 'wq_b', 'wk_w', 'wk_b', 'wv_w', 'wv_b', 'wc_w', 'wc_b')}
    del _L0_xattn_all

    def _L0_ffn_setup():
        import jax, jax.numpy as jnp
        import numpy as np
        B, S, D, E, F = (2, 256, 128, 8, 512)
        key = jax.random.key(seed)
        ks = jax.random.split(key, 4)
        return {'hidden_states': jax.random.normal(ks[0], (B, S, D), dtype=jnp.float32), 'Wr': jax.random.normal(ks[1], (D, E), dtype=jnp.float32) * (1.0 / np.sqrt(D)), 'W1': jax.random.normal(ks[2], (E, D, F), dtype=jnp.float32) * (1.0 / np.sqrt(D)), 'b1': jnp.zeros((E, F), dtype=jnp.float32), 'W2': jax.random.normal(ks[3], (E, F, D), dtype=jnp.float32) * (1.0 / np.sqrt(F)), 'b2': jnp.zeros((E, D), dtype=jnp.float32)}
    _L0_ffn_all = _L0_ffn_setup()
    _L0_ffn_in = {k: v for k, v in _L0_ffn_all.items() if k in ('Wr', 'W1', 'b1', 'W2', 'b2')}
    del _L0_ffn_all
    return {'x': x, 'ctx_1024': ctx_1024, 'g_xattn': g_xattn, 'g_ffn': g_ffn, 'L0_xattn_wq_w': _L0_xattn_in['wq_w'], 'L0_xattn_wq_b': _L0_xattn_in['wq_b'], 'L0_xattn_wk_w': _L0_xattn_in['wk_w'], 'L0_xattn_wk_b': _L0_xattn_in['wk_b'], 'L0_xattn_wv_w': _L0_xattn_in['wv_w'], 'L0_xattn_wv_b': _L0_xattn_in['wv_b'], 'L0_xattn_wc_w': _L0_xattn_in['wc_w'], 'L0_xattn_wc_b': _L0_xattn_in['wc_b'], 'L0_ffn_Wr': _L0_ffn_in['Wr'], 'L0_ffn_W1': _L0_ffn_in['W1'], 'L0_ffn_b1': _L0_ffn_in['b1'], 'L0_ffn_W2': _L0_ffn_in['W2'], 'L0_ffn_b2': _L0_ffn_in['b2']}

def reference(x, ctx_1024, g_xattn, g_ffn, L0_xattn_wq_w, L0_xattn_wq_b, L0_xattn_wk_w, L0_xattn_wk_b, L0_xattn_wv_w, L0_xattn_wv_b, L0_xattn_wc_w, L0_xattn_wc_b, L0_ffn_Wr, L0_ffn_W1, L0_ffn_b1, L0_ffn_W2, L0_ffn_b2):
    import jax
    import jax.numpy as jnp

    def _L0_xattn_ref(v, k, q, wq_w, wq_b, wk_w, wk_b, wv_w, wv_b, wc_w, wc_b):
        import jax, jax.numpy as jnp
        import numpy as np
        B, L, D_MODEL, N_HEADS = (4, 1024, 128, 16)
        D_DEPTH = D_MODEL // N_HEADS

        def _split_heads(x):
            b, l, _ = x.shape
            return x.reshape(b, l, N_HEADS, D_DEPTH).transpose(0, 2, 1, 3)

        def _combine_heads(x):
            b, _, l, _ = x.shape
            return x.transpose(0, 2, 1, 3).reshape(b, l, D_MODEL)
        q_heads = jax.nn.elu(_split_heads(q @ wq_w + wq_b)) + 1.0
        k_heads = jax.nn.elu(_split_heads(k @ wk_w + wk_b)) + 1.0
        v_heads = _split_heads(v @ wv_w + wv_b)
        k_cumsum = jnp.cumsum(k_heads, axis=1)
        attn_free = q_heads * (k_heads / k_cumsum) * v_heads
        return _combine_heads(attn_free) @ wc_w + wc_b

    def _L0_ffn_ref(hidden_states, Wr, W1, b1, W2, b2):
        import jax, jax.numpy as jnp
        import numpy as np
        B, S, D, E, F = (2, 256, 128, 8, 512)
        b, s, d = hidden_states.shape
        e = Wr.shape[1]
        x = hidden_states.reshape(b * s, d)
        router_logits = x @ Wr
        router_probs = jax.nn.softmax(router_logits, axis=-1)
        expert_idx = jnp.argmax(router_probs, axis=-1)
        p_max = jnp.max(router_probs, axis=-1, keepdims=True)

        def expert_mlp(w1, bb1, w2, bb2):
            h = jax.nn.gelu(x @ w1 + bb1, approximate=False)
            return h @ w2 + bb2
        outs = jax.vmap(expert_mlp)(W1, b1, W2, b2)
        onehot = jax.nn.one_hot(expert_idx, e, dtype=x.dtype)
        next_states = jnp.einsum('te,etd->td', onehot, outs)
        out = p_max * next_states
        return out.reshape(b, s, d)
    x = x + jnp.tanh(g_xattn[0]) * _L0_xattn_ref(ctx_1024, ctx_1024, _layernorm(x, axis=-1), L0_xattn_wq_w, L0_xattn_wq_b, L0_xattn_wk_w, L0_xattn_wk_b, L0_xattn_wv_w, L0_xattn_wv_b, L0_xattn_wc_w, L0_xattn_wc_b)
    x = x + jnp.tanh(g_ffn[0]) * _L0_ffn_ref(_layernorm(x, axis=-1), L0_ffn_Wr, L0_ffn_W1, L0_ffn_b1, L0_ffn_W2, L0_ffn_b2)
    return x

_drawn_inputs = setup_inputs


def setup_inputs(seed=0):
    import zlib

    import numpy as np

    out = dict(_drawn_inputs(seed))
    spreads = {'L0_xattn_wq_b': (0.0, 0.27),
     'L0_xattn_wk_b': (0.0, 0.34),
     'L0_xattn_wv_b': (0.0, 0.1),
     'L0_xattn_wc_b': (0.0, 0.1),
     'L0_ffn_b1': (0.0, 0.345),
     'L0_ffn_b2': (0.0, 0.1)}
    factors = {}
    for name, (base, spread) in spreads.items():
        noise = np.random.default_rng([zlib.crc32(name.encode()), seed]).standard_normal(out[name].shape)
        drawn = base * np.exp(spread * noise) if base else spread * noise
        out[name] = jnp.asarray(drawn.astype(out[name].dtype))
    for name, factor in factors.items():
        out[name] = (out[name] * factor).astype(out[name].dtype)
    return out
```

```python
from contextlib import ExitStack

import concourse.bass as bass
from concourse import mybir

ALU = mybir.AluOpType
ACT = mybir.ActivationFunctionType
F32 = mybir.dt.float32
BF16 = mybir.dt.bfloat16
I32 = mybir.dt.int32
U32 = mybir.dt.uint32
AX_X = mybir.AxisListType.X

P = 128
HEADS = 16
EPS = 1e-5
NO_TOKEN = 65535


def gated_block_kernel(nc, x, ctx, g_xattn, g_ffn, wq, bq, wk, bk, wv, bv, wc, bc, wr, w1, b1, w2, b2, out):
    B, S, D = x.shape
    E, _, F = w1.shape
    T = B * S
    NT = T // P
    NH = 2
    TH = NT // NH
    W = TH * P
    FC = F // P
    BLOCKS = (T + E * (P - 1)) // P
    GROUPS = [(0, 4), (4, 8), (8, 12), (12, BLOCKS)]
    MU, RS, GATE, ID, ROW = D, D + 1, D + 2, D + 3, D + 4
    NB = F + D
    assert S == P and D == P and W == 512 and F == 512 and BLOCKS == 15 and E == 8

    x_rows = x.rearrange("b p d -> p b d")
    ctx_rows = ctx.rearrange("b p d -> p b d")
    out_rows = out.rearrange("b p d -> (b p) d")
    slots = nc.dram_tensor("slots", (BLOCKS * P, ROW), F32).ap()

    with ExitStack() as stack:
        def sb(name, shape, dt=F32):
            return stack.enter_context(nc.sbuf_tensor(name, shape, dt))

        def sem(name):
            return stack.enter_context(nc.semaphore(name))

        x_sb = sb("x_sb", [P, NT, D])
        c_sb = sb("c_sb", [P, NT, D])
        wq_sb, wk_sb, wv_sb, wc_sb = (sb(n, [P, D]) for n in ("wq_sb", "wk_sb", "wv_sb", "wc_sb"))
        wr_sb = sb("wr_sb", [P, E])
        bq_sb, bk_sb, bv_sb = (sb(n, [P, 1]) for n in ("bq_sb", "bk_sb", "bv_sb"))
        bc_sb = sb("bc_sb", [P, D])
        g_sb = sb("g_sb", [P, 2])
        be_sb = sb("be_sb", [E, NB])
        w2_sb = sb("w2_sb", [P, E, FC, D])
        diff = sb("diff", [P, P])
        ident = sb("ident", [P, P])
        diff_i = sb("diff_i", [P, P], I32)
        depth_diff = sb("depth_diff", [P, P], I32)
        same_depth = sb("same_depth", [P, P])
        minus_half = sb("minus_half", [P, TH])
        head_sum = sb("head_sum", [P, P])
        before = sb("before", [P, P], BF16)
        ones = sb("ones", [P, P], BF16)
        rev = sb("rev", [P, E])
        ediff = sb("ediff", [P, E, E])
        earlier = sb("earlier", [P, E, E])
        first_slot = sb("first_slot", [1, BLOCKS])
        no_rows = sb("no_rows", [P, BLOCKS * ROW], U32)
        stats = sb("stats", [P, NT, 6])
        mv = sb("mv", [P, NT, 2])
        xn = sb("xn", [P, NT, D])
        tg = sb("tg", [P, 2])
        xb = sb("xb", [P, NT, D])
        cT, xnT, kexp, krelu, qexp, qrelu, kf, qf, inv, share, qk, attn = (
            sb(n, [P, T]) for n in ("cT", "xnT", "kexp", "krelu", "qexp", "qrelu", "kf", "qf", "inv", "share", "qk", "attn"))
        rows = sb("rows", [P, NT, ROW])
        stats2 = sb("stats2", [P, NT, 6])
        xn2 = sb("xn2", [P, NT, D])
        xn2T = sb("xn2T", [P, T])
        logit = sb("logit", [P, NT, E])
        top = sb("top", [P, NT])
        below = sb("below", [P, NT, E])
        expo = sb("expo", [P, NT, E])
        total = sb("total", [P, NT])
        pmax = sb("pmax", [P, NT])
        hit = sb("hit", [P, NT, E])
        score = sb("score", [P, NT, E])
        best = sb("best", [P, NT])
        onehot = sb("onehot", [P, NT, E], BF16)
        padded = sb("padded", [P, E], I32)
        room = sb("room", [P, E], I32)
        eprod = sb("eprod", [P, E, E])
        base = sb("base", [P, E])
        stop_of = sb("stop_of", [1, E])
        passed = sb("passed", [1, BLOCKS, E])
        eb_f = sb("eb_f", [1, BLOCKS])
        eb = sb("eb", [1, BLOCKS], I32)
        place = sb("place", [P, NT, E])
        placed = sb("placed", [P, NT, E])
        pos_f = sb("pos_f", [P, NT])
        pos = sb("pos", [P, NT], I32)
        b_hi, b_mid, b_lo = (sb(n, [E, NB], BF16) for n in ("b_hi", "b_mid", "b_lo"))
        b_r1 = sb("b_r1", [E, NB])
        b_r2 = sb("b_r2", [E, NB])
        b_parts = sb("b_parts", [3, E, NB], BF16)
        slot_rows = sb("slot_rows", [P, BLOCKS, ROW])
        sx = sb("sx", [P, BLOCKS, D])
        sxT = sb("sxT", [P, BLOCKS, P])
        w1_sb = sb("w1_sb", [P, 2, F])
        hid = sb("hid", [P, 2, FC, P])
        res = sb("res", [P, BLOCKS, D])

        ps = [stack.enter_context(nc.psum_tensor(f"ps{i}", [P, 512], F32)) for i in range(8)]

        x_in = [sem(f"x_in{h}") for h in range(NH)]
        c_in = [sem(f"c_in{h}") for h in range(NH)]
        wk_in, wq_in, wv_in, g_in, bc_in, wc_in, wr_in, be_in, bparts_in, w2_in = (
            sem(n) for n in ("wk_in", "wq_in", "wv_in", "g_in", "bc_in", "wc_in", "wr_in", "be_in", "bparts_in", "w2_in"))
        slots_cleared, slots_written = sem("slots_cleared"), sem("slots_written")
        rows_in = [sem(f"rows_in{g}") for g in range(len(GROUPS))]
        w1_in = [sem("w1_in0"), sem("w1_in1")]
        stored = sem("stored")
        diff_made, ident_made, masks_made, ones_made, norow_made, ids_made, iotas_made = (
            sem(n) for n in ("diff_made", "ident_made", "masks_made", "ones_made", "norow_made", "ids_made", "iotas_made"))
        half_made, eps_done, eps2_done = sem("half_made"), sem("eps_done"), sem("eps2_done")
        inv_done = sem("inv_done")
        depth_made, earlier_made = sem("depth_made"), sem("earlier_made")
        (st_done, mv_done, rstd_done, xn_done, cT_ps, cT_done, xnT_ps, xnT_done, k_ps, q_ps, v_ps, sum_ps,
         k_act, q_act, kf_done, qf_done, share_done, qk_done, attn_done, tg_done, xb_done, y_ps, x1_done) = (
            sem(n) for n in ("st_done", "mv_done", "rstd_done", "xn_done", "cT_ps", "cT_done", "xnT_ps", "xnT_done",
                             "k_ps", "q_ps", "v_ps", "sum_ps", "k_act", "q_act", "kf_done", "qf_done",
                             "share_done", "qk_done", "attn_done", "tg_done", "xb_done", "y_ps", "x1_done"))
        (st2_done, mv2_done, rstd2_done, xn2_done, xn2T_ps, xn2T_done, logit_ps, logit_done, top_done, below_done,
         expo_done, total_done, pmax_done, gate_done, hit_done, score_done, best_done, onehot_done, count_ps,
         route_step, eb_done, place_done, pos_done) = (
            sem(n) for n in ("st2_done", "mv2_done", "rstd2_done", "xn2_done", "xn2T_ps", "xn2T_done", "logit_ps",
                             "logit_done", "top_done", "below_done", "expo_done", "total_done", "pmax_done",
                             "gate_done", "hit_done", "score_done", "best_done", "onehot_done", "count_ps",
                             "route_step", "eb_done", "place_done", "pos_done"))
        bsplit, sx_done, sxT_ps, sxT_done, h_ps, hid_done, e_ps, res_done = (
            sem(n) for n in ("bsplit", "sx_done", "sxT_ps", "sxT_done", "h_ps", "hid_done", "e_ps", "res_done"))

        block = stack.enter_context(nc.Block())

        @block.sync
        def _(sp):
            for h in range(NH):
                t = slice(h * TH, (h + 1) * TH)
                sp.dma_start(x_sb[:, t, :], x_rows[:, t, :]).then_inc(x_in[h], 16)
                sp.dma_start(c_sb[:, t, :], ctx_rows[:, t, :]).then_inc(c_in[h], 16)
            sp.dma_start(wc_sb[:], wc).then_inc(wc_in, 16)
            sp.dma_start(wr_sb[:], wr).then_inc(wr_in, 16)
            sp.wait_ge(norow_made, 1)
            sp.dma_start(slots.rearrange("(p b) r -> p (b r)", p=P),
                         no_rows[:].bitcast(F32)).then_inc(slots_cleared, 16)
            sp.wait_ge(bsplit, 5)
            for j, part in enumerate((b_hi, b_mid, b_lo)):
                sp.dma_start(b_parts[j:j + 1, :, :], part[:]).then_inc(bparts_in, 16)
            sp.dma_start(w2_sb[:], w2.rearrange("e (c p) d -> p e c d", p=P)).then_inc(w2_in, 16)
            sp.wait_ge(slots_written, 16 * NT)
            for g, (a, z) in enumerate(GROUPS):
                sp.dma_start(slot_rows[:, a:z, :],
                             slots[a * P:z * P, :].rearrange("(b p) r -> p b r", p=P)).then_inc(rows_in[g], 16)

            def load_w1(b, u, used):
                e = sp.value_load(eb[0:1, bass.ds(b, 1)], min_val=0, max_val=E - 1)
                if used is not None:
                    sp.wait_ge(h_ps, used)
                sp.dma_start(w1_sb[:, u, :], w1[bass.ds(e, 1), :, :].rearrange("o d f -> d (o f)")).then_inc(w1_in[u], 16)

            sp.wait_ge(eb_done, 1)
            load_w1(0, 0, None)
            load_w1(1, 1, None)
            with sp.Fori(1, BLOCKS // 2) as i:
                for u in range(2):
                    load_w1(2 * i + u, u, 2 * i + u - 1)
            load_w1(BLOCKS - 1, 0, BLOCKS - 2)

        @block.gpsimd
        def _(pool):
            pool.iota(diff[:], [[1, P]], base=P, channel_multiplier=-1,
                      allow_small_or_imprecise_dtypes=True).then_inc(diff_made, 1)
            pool.memset(minus_half[:], -0.5).then_inc(half_made, 1)
            pool.memset(no_rows[:], NO_TOKEN).then_inc(norow_made, 1)
            pool.memset(ones[:], 1.0).then_inc(ones_made, 1)
            pool.iota(rows[:, :, ID].bitcast(I32), [[P, NT]], base=0, channel_multiplier=1).then_inc(ids_made, 1)
            pool.iota(rev[:], [[-1, E]], base=E, channel_multiplier=0,
                      allow_small_or_imprecise_dtypes=True).then_inc(iotas_made, 1)
            pool.iota(ediff[:], [[1, E], [-1, E]], base=0, channel_multiplier=0,
                      allow_small_or_imprecise_dtypes=True).then_inc(iotas_made, 1)
            pool.iota(first_slot[:], [[P, BLOCKS]], base=0, channel_multiplier=0,
                      allow_small_or_imprecise_dtypes=True).then_inc(iotas_made, 1)

            def rstd(h, var, var_done, eps_done, done):
                pool.wait_ge(var_done, (h + 1) * TH)
                pool.tensor_scalar(var, var, EPS, None, ALU.add).then_inc(eps_done, 1)
                pool.wait_ge(eps_done, h + 1)
                pool.tensor_tensor(var, var, minus_half[:], ALU.pow).then_inc(done, 1)

            pool.wait_ge(half_made, 1)
            for h in range(NH):
                rstd(h, mv[:, h * TH:(h + 1) * TH, 1], mv_done, eps_done, rstd_done)
            for h in range(NH):
                s = slice(h * W, (h + 1) * W)
                pool.wait_ge(inv_done, h + 1)
                pool.wait_ge(kf_done, h + 1)
                pool.tensor_tensor(share[:, s], kf[:, s], inv[:, s], ALU.mult).then_inc(share_done, 1)
                pool.wait_ge(qf_done, h + 1)
                pool.wait_ge(share_done, h + 1)
                pool.tensor_tensor(qk[:, s], qf[:, s], share[:, s], ALU.mult).then_inc(qk_done, 1)
            for h in range(NH):
                rstd(h, rows[:, h * TH:(h + 1) * TH, RS], mv2_done, eps2_done, rstd2_done)
            pool.wait_ge(slots_cleared, 16)
            pool.wait_ge(ids_made, 1)
            pool.wait_ge(gate_done, 1)
            pool.wait_ge(pos_done, 1)
            for t in range(NT):
                pool.indirect_dma_start(
                    out=slots, out_offset=bass.IndirectOffsetOnAxis(ap=pos[:, t:t + 1].bitcast(U32), axis=0),
                    in_=rows[:, t, :], in_offset=None).then_inc(slots_written, 16)
            for b in range(BLOCKS):
                pool.wait_ge(res_done, b + 1)
                pool.indirect_dma_start(
                    out=out_rows,
                    out_offset=bass.IndirectOffsetOnAxis(ap=slot_rows[:, b, ID:ID + 1].bitcast(U32), axis=0),
                    in_=res[:, b, :], in_offset=None, bounds_check=T - 1, oob_is_err=False).then_inc(stored, 16)
            pool.wait_ge(stored, 16 * BLOCKS)

        @block.scalar
        def _(act):
            act.dma_start(wk_sb[:], wk).then_inc(wk_in, 16)
            act.dma_start(bk_sb[:], bk.rearrange("(d o) -> d o", o=1)).then_inc(wk_in, 16)
            act.dma_start(wq_sb[:], wq).then_inc(wq_in, 16)
            act.dma_start(bq_sb[:], bq.rearrange("(d o) -> d o", o=1)).then_inc(wq_in, 16)
            act.dma_start(wv_sb[:], wv).then_inc(wv_in, 16)
            act.dma_start(bv_sb[:], bv.rearrange("(d o) -> d o", o=1)).then_inc(wv_in, 16)
            act.dma_start(g_sb[:, 0:1], g_xattn.partition_broadcast(P)).then_inc(g_in, 16)
            act.dma_start(g_sb[:, 1:2], g_ffn.partition_broadcast(P)).then_inc(g_in, 16)
            act.dma_start(bc_sb[:], bc.partition_broadcast(P)).then_inc(bc_in, 16)
            act.dma_start(be_sb[:, 0:F], b1).then_inc(be_in, 16)
            act.dma_start(be_sb[:, F:NB], b2).then_inc(be_in, 16)
            act.wait_ge(g_in, 32)
            act.activation(tg[:], g_sb[:], ACT.Tanh).then_inc(tg_done, 1)
            for h in range(NH):
                s = slice(h * W, (h + 1) * W)
                act.wait_ge(cT_ps, h + 1)
                act.activation(cT[:, s], ps[4 * h][:], ACT.Copy).then_inc(cT_done, 1)
                act.wait_ge(k_ps, h + 1)
                act.wait_ge(wk_in, 32)
                act.activation(kexp[:, s], ps[4 * h + 2][:], ACT.Exp, bias=bk_sb[:]).then_inc(k_act, 1)
                act.activation(krelu[:, s], ps[4 * h + 2][:], ACT.Relu, bias=bk_sb[:]).then_inc(k_act, 1)
                act.wait_ge(q_ps, h + 1)
                act.wait_ge(wq_in, 32)
                act.activation(qexp[:, s], ps[4 * h + 3][:], ACT.Exp, bias=bq_sb[:]).then_inc(q_act, 1)
                act.activation(qrelu[:, s], ps[4 * h + 3][:], ACT.Relu, bias=bq_sb[:]).then_inc(q_act, 1)
            for h in range(NH):
                s = slice(h * W, (h + 1) * W)
                act.wait_ge(xn2T_ps, h + 1)
                act.activation(xn2T[:, s], ps[4 * h + 3][:], ACT.Copy).then_inc(xn2T_done, 1)
            act.wait_ge(below_done, 1)
            act.activation(expo[:], below[:], ACT.Exp).then_inc(expo_done, 1)
            for g, (a, z) in enumerate(GROUPS):
                act.wait_ge(sxT_ps, g + 1)
                act.activation(sxT[:, a:z, :], ps[4 + g][:, 0:(z - a) * P].rearrange("p (b s) -> p b s", s=P),
                               ACT.Copy).then_inc(sxT_done, 1)

            def gelu(b, u):
                act.wait_ge(h_ps, b + 1)
                act.activation(hid[:, u, :, :], ps[u][:].rearrange("p (c s) -> p c s", c=FC),
                               ACT.Gelu).then_inc(hid_done, 1)

            gelu(0, 0)
            gelu(1, 1)
            with act.Fori(1, BLOCKS // 2) as i:
                for u in range(2):
                    act.wait_ge(e_ps, 2 * i + u - 1)
                    gelu(2 * i + u, u)
            act.wait_ge(e_ps, BLOCKS - 2)
            gelu(BLOCKS - 1, 0)

        @block.vector
        def _(dve):
            dve.wait_ge(diff_made, 1)
            dve.tensor_scalar(ident[:], diff[:], float(P), None, ALU.is_equal).then_inc(ident_made, 1)
            dve.tensor_copy(diff_i[:], diff[:]).then_inc(depth_made, 1)
            dve.wait_ge(depth_made, 1)
            dve.tensor_scalar(depth_diff[:], diff_i[:], D // HEADS - 1, None, ALU.bitwise_and).then_inc(depth_made, 1)
            dve.wait_ge(depth_made, 2)
            dve.tensor_scalar(same_depth[:], depth_diff[:], 0.0, None, ALU.is_equal).then_inc(depth_made, 1)
            dve.tensor_scalar(before[:], diff[:], float(P), None, ALU.is_gt).then_inc(masks_made, 1)

            for h in range(NH):
                dve.wait_ge(x_in[h], 16)
                for t in range(h * TH, (h + 1) * TH):
                    dve.bn_stats(stats[:, t, :], x_sb[:, t, :]).then_inc(st_done, 1)
                for t in range(h * TH, (h + 1) * TH):
                    dve.wait_ge(st_done, t + 1)
                    dve.bn_aggr(mv[:, t, :], stats[:, t, :]).then_inc(mv_done, 1)
                ts = slice(h * TH, (h + 1) * TH)
                dve.wait_ge(rstd_done, h + 1)
                for t in range(h * TH, (h + 1) * TH):
                    last = dve.tensor_scalar(xn[:, t, :], x_sb[:, t, :], mv[:, t, 0:1], mv[:, t, 1:2],
                                             ALU.subtract, ALU.mult)
                last.then_inc(xn_done, 1)
            dve.wait_ge(depth_made, 3)
            dve.scalar_tensor_tensor(head_sum[:], diff[:], float(P), same_depth[:], ALU.is_ge, ALU.mult).then_inc(masks_made, 1)
            dve.wait_ge(tg_done, 1)
            dve.wait_ge(bc_in, 16)
            for h in range(NH):
                ts = slice(h * TH, (h + 1) * TH)
                s = slice(h * W, (h + 1) * W)
                A, Bk, C = ps[4 * h], ps[4 * h + 1], ps[4 * h + 2]
                dve.wait_ge(xnT_ps, h + 1)
                dve.tensor_copy(xnT[:, s], Bk[:]).then_inc(xnT_done, 1)
                dve.scalar_tensor_tensor(xb[:, ts, :], bc_sb[:].unsqueeze(1).broadcast_to([P, TH, D]), tg[:, 0:1],
                                         x_sb[:, ts, :], ALU.mult, ALU.add).then_inc(xb_done, 1)
                dve.wait_ge(k_act, 2 * h + 2)
                dve.scalar_tensor_tensor(kf[:, s], kexp[:, s], 1.0, krelu[:, s], ALU.min, ALU.add).then_inc(kf_done, 1)
                dve.wait_ge(q_act, 2 * h + 2)
                dve.scalar_tensor_tensor(qf[:, s], qexp[:, s], 1.0, qrelu[:, s], ALU.min, ALU.add).then_inc(qf_done, 1)
            for h in range(NH):
                dve.wait_ge(sum_ps, h + 1)
                dve.reciprocal(inv[:, h * W:(h + 1) * W], ps[4 * h + 1][:]).then_inc(inv_done, 1)
            dve.wait_ge(wv_in, 32)
            for h in range(NH):
                ts = slice(h * TH, (h + 1) * TH)
                s = slice(h * W, (h + 1) * W)
                A, Bk, C = ps[4 * h], ps[4 * h + 1], ps[4 * h + 2]
                dve.wait_ge(v_ps, h + 1)
                dve.wait_ge(qk_done, h + 1)
                dve.scalar_tensor_tensor(attn[:, s], A[:], bv_sb[:], qk[:, s], ALU.add, ALU.mult).then_inc(attn_done, 1)
            for h in range(NH):
                ts = slice(h * TH, (h + 1) * TH)
                C = ps[4 * h + 2]
                dve.wait_ge(y_ps, h + 1)
                dve.wait_ge(xb_done, h + 1)
                dve.scalar_tensor_tensor(rows[:, ts, 0:D], C[:].rearrange("p (t d) -> p t d", d=D), tg[:, 0:1],
                                         xb[:, ts, :], ALU.mult, ALU.add).then_inc(x1_done, 1)
                dve.wait_ge(x1_done, h + 1)
                for t in range(h * TH, (h + 1) * TH):
                    dve.bn_stats(stats2[:, t, :], rows[:, t, 0:D]).then_inc(st2_done, 1)
                for t in range(h * TH, (h + 1) * TH):
                    dve.wait_ge(st2_done, t + 1)
                    dve.bn_aggr(rows[:, t, MU:MU + 2], stats2[:, t, :]).then_inc(mv2_done, 1)
                dve.wait_ge(rstd2_done, h + 1)
                for t in range(h * TH, (h + 1) * TH):
                    last = dve.tensor_scalar(xn2[:, t, :], rows[:, t, 0:D], rows[:, t, MU:MU + 1], rows[:, t, RS:RS + 1],
                                             ALU.subtract, ALU.mult)
                last.then_inc(xn2_done, 1)
            dve.wait_ge(be_in, 32)
            dve.tensor_copy(b_hi[:], be_sb[:]).then_inc(bsplit, 1)
            dve.wait_ge(bsplit, 1)
            dve.tensor_tensor(b_r1[:], be_sb[:], b_hi[:], ALU.subtract).then_inc(bsplit, 1)
            dve.wait_ge(bsplit, 2)
            dve.tensor_copy(b_mid[:], b_r1[:]).then_inc(bsplit, 1)
            dve.wait_ge(bsplit, 3)
            dve.tensor_tensor(b_r2[:], b_r1[:], b_mid[:], ALU.subtract).then_inc(bsplit, 1)
            dve.wait_ge(bsplit, 4)
            dve.tensor_copy(b_lo[:], b_r2[:]).then_inc(bsplit, 1)
            dve.wait_ge(iotas_made, 3)
            dve.tensor_scalar(earlier[:], ediff[:], 0.0, None, ALU.is_gt).then_inc(earlier_made, 1)

            te = [P, NT, E]
            for h in range(NH):
                dve.wait_ge(logit_ps, h + 1)
                dve.tensor_copy(logit[:, h * TH:(h + 1) * TH, :],
                                ps[4 * h][:, 0:TH * E].rearrange("p (t e) -> p t e", e=E)).then_inc(logit_done, 1)
            dve.wait_ge(logit_done, NH)
            dve.reduce_max(top[:], logit[:], AX_X).then_inc(top_done, 1)
            dve.wait_ge(top_done, 1)
            dve.tensor_tensor(hit[:], logit[:], top[:].unsqueeze(2).broadcast_to(te), ALU.is_equal).then_inc(hit_done, 1)
            dve.tensor_tensor(below[:], logit[:], top[:].unsqueeze(2).broadcast_to(te), ALU.subtract).then_inc(below_done, 1)
            dve.wait_ge(hit_done, 1)
            dve.tensor_tensor(score[:], hit[:], rev[:].unsqueeze(1).broadcast_to(te), ALU.mult).then_inc(score_done, 1)
            dve.wait_ge(score_done, 1)
            dve.reduce_max(best[:], score[:], AX_X).then_inc(best_done, 1)
            dve.wait_ge(best_done, 1)
            dve.tensor_tensor(onehot[:], score[:], best[:].unsqueeze(2).broadcast_to(te), ALU.is_equal).then_inc(onehot_done, 1)
            dve.wait_ge(expo_done, 1)
            dve.reduce_sum(total[:], expo[:], AX_X).then_inc(total_done, 1)
            dve.wait_ge(total_done, 1)
            dve.reciprocal(pmax[:], total[:]).then_inc(pmax_done, 1)
            dve.wait_ge(pmax_done, 1)
            dve.tensor_scalar(rows[:, :, GATE], pmax[:], tg[:, 1:2], None, ALU.mult).then_inc(gate_done, 1)
            rank, many = ps[1][:, 0:NT * E], ps[1][:, NT * E:NT * E + E]
            dve.wait_ge(count_ps, 1)
            dve.tensor_scalar(padded[:], many, float(P - 1), None, ALU.add).then_inc(route_step, 1)
            dve.wait_ge(route_step, 1)
            dve.tensor_scalar(room[:], padded[:], 7, 7, ALU.logical_shift_right, ALU.logical_shift_left).then_inc(route_step, 1)
            dve.wait_ge(route_step, 2)
            dve.wait_ge(earlier_made, 1)
            dve.tensor_tensor(eprod[:], earlier[:], room[:].unsqueeze(1).broadcast_to([P, E, E]), ALU.mult).then_inc(route_step, 1)
            dve.wait_ge(route_step, 3)
            dve.reduce_sum(base[:], eprod[:], AX_X).then_inc(route_step, 1)
            dve.wait_ge(route_step, 4)
            dve.tensor_tensor(place[:], rank.rearrange("p (t e) -> p t e", e=E),
                              base[:].unsqueeze(1).broadcast_to(te), ALU.add).then_inc(route_step, 1)
            dve.wait_ge(route_step, 5)
            dve.tensor_tensor(placed[:], place[:], onehot[:], ALU.mult).then_inc(route_step, 1)
            dve.wait_ge(route_step, 6)
            dve.reduce_sum(pos_f[:], placed[:], AX_X).then_inc(route_step, 1)
            dve.wait_ge(route_step, 7)
            dve.tensor_copy(pos[:], pos_f[:]).then_inc(pos_done, 1)
            be = [1, BLOCKS, E]
            dve.tensor_tensor(stop_of[:], base[0:1, :], room[0:1, :], ALU.add).then_inc(route_step, 1)
            dve.wait_ge(route_step, 8)
            dve.tensor_tensor(passed[:], stop_of[:].unsqueeze(1).broadcast_to(be),
                              first_slot[:].unsqueeze(2).broadcast_to(be), ALU.is_le).then_inc(route_step, 1)
            dve.wait_ge(route_step, 9)
            dve.reduce_sum(eb_f[:], passed[:], AX_X).then_inc(route_step, 1)
            dve.wait_ge(route_step, 10)
            dve.tensor_scalar(eb[:], eb_f[:], float(E - 1), None, ALU.min).then_inc(eb_done, 1)

            for g, (a, z) in enumerate(GROUPS):
                dve.wait_ge(rows_in[g], 16)
                for b in range(a, z):
                    last = dve.tensor_scalar(sx[:, b, :], slot_rows[:, b, 0:D], slot_rows[:, b, MU:MU + 1],
                                             slot_rows[:, b, RS:RS + 1], ALU.subtract, ALU.mult)
                last.then_inc(sx_done, 1)

            def residual(b, u):
                dve.wait_ge(e_ps, b + 1)
                dve.scalar_tensor_tensor(res[:, bass.ds(b, 1), :].rearrange("p o d -> p (o d)"), ps[2 + u][:, 0:D],
                                         slot_rows[:, bass.ds(b, 1), GATE],
                                         slot_rows[:, bass.ds(b, 1), 0:D].rearrange("p o d -> p (o d)"),
                                         ALU.mult, ALU.add).then_inc(res_done, 1)

            with dve.Fori(0, BLOCKS // 2) as i:
                for u in range(2):
                    residual(2 * i + u, u)
            residual(BLOCKS - 1, 0)

        @block.tensor
        def _(pe):
            def turn(dst, src):
                return pe.transpose(dst, src, ident[:])

            pe.wait_ge(ident_made, 1)
            for h in range(NH):
                A, Bk, C, Q = (ps[4 * h + j] for j in range(4))
                s = slice(h * W, (h + 1) * W)
                pe.wait_ge(c_in[h], 16)
                for t in range(TH):
                    mm = turn(A[:, t * P:(t + 1) * P], c_sb[:, h * TH + t, :])
                mm.then_inc(cT_ps, 1)
                pe.wait_ge(xn_done, h + 1)
                for t in range(TH):
                    mm = turn(Bk[:, t * P:(t + 1) * P], xn[:, h * TH + t, :])
                mm.then_inc(xnT_ps, 1)
                pe.wait_ge(cT_done, h + 1)
                pe.wait_ge(wk_in, 32)
                pe.matmul(C[:], wk_sb[:], cT[:, s], start=True, stop=True).then_inc(k_ps, 1)
                pe.wait_ge(xnT_done, h + 1)
                pe.wait_ge(wq_in, 32)
                pe.matmul(Q[:], wq_sb[:], xnT[:, s], start=True, stop=True).then_inc(q_ps, 1)
                pe.wait_ge(wv_in, 32)
                pe.matmul(A[:], wv_sb[:], cT[:, s], start=True, stop=True).then_inc(v_ps, 1)
            pe.wait_ge(masks_made, 2)
            for h in range(NH):
                s = slice(h * W, (h + 1) * W)
                pe.wait_ge(kf_done, h + 1)
                pe.matmul(ps[4 * h + 1][:], head_sum[:], kf[:, s], start=True, stop=True).then_inc(sum_ps, 1)
            pe.wait_ge(wc_in, 16)
            for h in range(NH):
                pe.wait_ge(attn_done, h + 1)
                for t in range(TH):
                    mm = pe.matmul(ps[4 * h + 2][:, t * P:(t + 1) * P], attn[:, (h * TH + t) * P:(h * TH + t + 1) * P],
                                   wc_sb[:], start=True, stop=True)
                mm.then_inc(y_ps, 1)
            pe.wait_ge(wr_in, 16)
            for h in range(NH):
                pe.wait_ge(xn2_done, h + 1)
                for t in range(TH):
                    mm = turn(ps[4 * h + 3][:, t * P:(t + 1) * P], xn2[:, h * TH + t, :])
                mm.then_inc(xn2T_ps, 1)
                pe.wait_ge(xn2T_done, h + 1)
                for t in range(TH):
                    mm = pe.matmul(ps[4 * h][:, t * E:(t + 1) * E], xn2T[:, (h * TH + t) * P:(h * TH + t + 1) * P],
                                   wr_sb[:], start=True, stop=True)
                mm.then_inc(logit_ps, 1)
            pe.wait_ge(ones_made, 1)
            pe.wait_ge(onehot_done, 1)
            R = ps[1]
            pe.matmul(R[:, 0:NT * E], before[:], onehot[:], start=True, stop=True)
            for t in range(NT - 1):
                later = NT - 1 - t
                pe.matmul(R[:, (t + 1) * E:NT * E].rearrange("p (t e) -> p t e", e=E), ones[:],
                          onehot[:, t:t + 1, :].broadcast_to([P, later, E]),
                          start=False, stop=True, skip_group_check=True)
            for t in range(NT):
                mm = pe.matmul(R[:, NT * E:NT * E + E], ones[:], onehot[:, t, :], start=(t == 0), stop=(t == NT - 1))
            mm.then_inc(count_ps, 1)

            for g, (a, z) in enumerate(GROUPS):
                pe.wait_ge(sx_done, g + 1)
                for b in range(a, z):
                    mm = turn(ps[4 + g][:, (b - a) * P:(b - a + 1) * P], sx[:, b, :])
                mm.then_inc(sxT_ps, 1)

            def hidden(b, u, nth):
                e = pe.value_load(eb[0:1, bass.ds(b, 1)], min_val=0, max_val=E - 1)
                pe.wait_ge(w1_in[u], 16 * nth)
                for c in range(FC):
                    to = ps[u][:, c * P:(c + 1) * P]
                    pe.matmul(to, b_parts[:, bass.ds(e, 1), c * P:(c + 1) * P].rearrange("k o f -> k (o f)"),
                              ones[0:3, :], start=True, stop=False)
                    mm = pe.matmul(to, w1_sb[:, u, c * P:(c + 1) * P],
                                   sxT[:, bass.ds(b, 1), :].rearrange("p o s -> p (o s)"), start=False, stop=True)
                mm.then_inc(h_ps, 1)

            def result(b, u, read):
                e = pe.value_load(eb[0:1, bass.ds(b, 1)], min_val=0, max_val=E - 1)
                to = ps[2 + u][:, 0:D]
                if read is not None:
                    pe.wait_ge(res_done, read)
                pe.matmul(to, ones[0:3, :], b_parts[:, bass.ds(e, 1), F:NB].rearrange("k o f -> k (o f)"),
                          start=True, stop=False)
                pe.wait_ge(hid_done, b + 1)
                for c in range(FC):
                    mm = pe.matmul(to, hid[:, u, c, :], w2_sb[:, bass.ds(e, 1), c, :].rearrange("p o d -> p (o d)"),
                                   start=False, stop=(c == FC - 1))
                mm.then_inc(e_ps, 1)

            pe.wait_ge(eb_done, 1)
            pe.wait_ge(bparts_in, 48)
            pe.wait_ge(w2_in, 16)
            pe.wait_ge(sxT_done, len(GROUPS))
            hidden(0, 0, 1)
            hidden(1, 1, 1)
            result(0, 0, None)
            hidden(2, 0, 2)
            result(1, 1, None)
            with pe.Fori(1, BLOCKS // 2) as i:
                hidden(2 * i + 1, 1, i + 1)
                result(2 * i, 0, 2 * i - 1)
                hidden(2 * i + 2, 0, i + 2)
                result(2 * i + 1, 1, 2 * i)
            result(BLOCKS - 1, 0, BLOCKS - 2)


_INS = ['x', 'ctx_1024', 'g_xattn', 'g_ffn', 'L0_xattn_wq_w', 'L0_xattn_wq_b', 'L0_xattn_wk_w', 'L0_xattn_wk_b',
        'L0_xattn_wv_w', 'L0_xattn_wv_b', 'L0_xattn_wc_w', 'L0_xattn_wc_b', 'L0_ffn_Wr', 'L0_ffn_W1', 'L0_ffn_b1',
        'L0_ffn_W2', 'L0_ffn_b2']
_OUTS = [((8, 128, 128), 'float32')]


def kernel(**inputs):
    import numpy as _np
    import concourse.bacc as _bacc
    from concourse import mybir as _mybir
    from concourse.bass_utils import run_bass_kernel_spmd as _run

    nc = _bacc.Bacc("TRN2", target_bir_lowering=False, num_devices=1)
    arrays, args = {}, []
    for name in _INS:
        a = _np.ascontiguousarray(inputs[name])
        arrays[f"in_{name}_dram"] = a
        args.append(nc.dram_tensor(f"in_{name}_dram", a.shape, _mybir.dt.from_np(a.dtype), kind="ExternalInput").ap())
    for i, (shape, dtype) in enumerate(_OUTS):
        dt = _mybir.dt.from_np(_np.dtype(dtype))
        args.append(nc.dram_tensor(f"out_{i}_dram", shape, dt, kind="ExternalOutput").ap())
    gated_block_kernel(nc, *args)
    r = _run(nc, [arrays], core_ids=[0])
    return r.results[0]["out_0_dram"]
```

```python
from contextlib import ExitStack

import concourse.bass as bass
from concourse import mybir

ALU = mybir.AluOpType
ACT = mybir.ActivationFunctionType
F32 = mybir.dt.float32
BF16 = mybir.dt.bfloat16
I32 = mybir.dt.int32
U32 = mybir.dt.uint32
AX_X = mybir.AxisListType.X

P = 128
HEADS = 16
EPS = 1e-5
NO_TOKEN = 65535


def gated_block_kernel(nc, x, ctx, kq_params, vcr_params, expert_biases, w1, w2, out):
    B, S, D = x.shape
    E, _, F = w1.shape
    T = B * S
    NT = T // P
    NH = 2
    TH = NT // NH
    W = TH * P
    FC = F // P
    BLOCKS = (T + E * (P - 1)) // P
    RING = 3
    G = BLOCKS // RING
    MU, RS, GATE, ID, ROW = D, D + 1, D + 2, D + 3, D + 4
    NB = F + D
    BP, BROWS = 32, 72
    assert S == P and D == P and W == 512 and F == 512 and BLOCKS == G * RING and E == 8

    x_rows = x.rearrange("b p d -> p b d")
    ctx_rows = ctx.rearrange("b p d -> p b d")
    out_rows = out.rearrange("b p d -> (b p) d")
    slots = nc.dram_tensor("slots", (BLOCKS * P, ROW), F32).ap()

    with ExitStack() as stack:
        def sb(name, shape, dt=F32):
            return stack.enter_context(nc.sbuf_tensor(name, shape, dt))

        def sem(name):
            return stack.enter_context(nc.semaphore(name))

        x_sb = sb("x_sb", [P, NT, D])
        c_sb = sb("c_sb", [P, NT, D])
        kq_sb = sb("kq_sb", [P, 2 * D + 4])
        wk_sb, wq_sb = kq_sb[:, 0:D], kq_sb[:, D:2 * D]
        bk_sb, bq_sb, g_sb = kq_sb[:, 2 * D:2 * D + 1], kq_sb[:, 2 * D + 1:2 * D + 2], kq_sb[:, 2 * D + 2:2 * D + 4]
        vcr_sb = sb("vcr_sb", [P, 3 * D + E + 1])
        wv_sb, wc_sb, wr_sb = vcr_sb[:, 0:D], vcr_sb[:, D:2 * D], vcr_sb[:, 2 * D:2 * D + E]
        bv_sb, bc_sb = vcr_sb[:, 2 * D + E:2 * D + E + 1], vcr_sb[:, 2 * D + E + 1:3 * D + E + 1]
        be_sb = sb("be_sb", [BROWS, NB])
        w2_sb = sb("w2_sb", [P, E, FC, D])
        diff = sb("diff", [P, P])
        ident = sb("ident", [P, P])
        diff_i = sb("diff_i", [P, P], I32)
        depth_diff = sb("depth_diff", [P, P], I32)
        same_depth = sb("same_depth", [P, P])
        minus_half = sb("minus_half", [P, TH])
        head_sum = sb("head_sum", [P, P])
        before = sb("before", [P, P], BF16)
        ones = sb("ones", [P, P], BF16)
        rev = sb("rev", [P, E])
        ediff = sb("ediff", [P, E, E])
        earlier = sb("earlier", [P, E, E])
        first_slot = sb("first_slot", [P, BLOCKS])
        row_no = sb("row_no", [BROWS, 1], I32)
        row_low = sb("row_low", [BROWS, 1], I32)
        row_e = sb("row_e", [BROWS, 1])
        no_rows = sb("no_rows", [P, BLOCKS * ROW], U32)
        stats = sb("stats", [P, NT, 6])
        mv = sb("mv", [P, NT, 2])
        xn = sb("xn", [P, NT, D])
        tg = sb("tg", [P, 2])
        xb = sb("xb", [P, NT, D])
        cT, xnT, kexp, krelu, qexp, qrelu, kf, qf, inv, share, qk, attn = (
            sb(n, [P, T]) for n in ("cT", "xnT", "kexp", "krelu", "qexp", "qrelu", "kf", "qf", "inv", "share", "qk", "attn"))
        gated_bc = sb("gated_bc", [P, D])
        rows = sb("rows", [P, NT, ROW])
        stats2 = sb("stats2", [P, NT, 6])
        xn2 = sb("xn2", [P, NT, D])
        xn2T = sb("xn2T", [P, T])
        logit = sb("logit", [P, NT, E])
        top = sb("top", [P, NT])
        below = sb("below", [P, NT, E])
        expo = sb("expo", [P, NT, E])
        total = sb("total", [P, NT])
        pmax = sb("pmax", [P, NT])
        hit = sb("hit", [P, NT, E])
        score = sb("score", [P, NT, E])
        best = sb("best", [P, NT])
        onehot = sb("onehot", [P, NT, E], BF16)
        padded = sb("padded", [P, E], I32)
        room = sb("room", [P, E], I32)
        eprod = sb("eprod", [P, E, E])
        base = sb("base", [P, E])
        stop_of = sb("stop_of", [P, E])
        passed = sb("passed", [P, BLOCKS, E])
        eb_f = sb("eb_f", [P, BLOCKS])
        b_select = sb("b_select", [BROWS, BLOCKS], BF16)
        eb = sb("eb", [1, BLOCKS], I32)
        place = sb("place", [P, NT, E])
        placed = sb("placed", [P, NT, E])
        pos_f = sb("pos_f", [P, NT])
        pos = sb("pos", [P, NT], I32)
        b_parts = sb("b_parts", [BROWS, NB], BF16)
        b_mid = sb("b_mid", [BROWS, NB], BF16)
        b_rest = sb("b_rest", [BROWS, NB])
        slot_rows = sb("slot_rows", [P, BLOCKS, ROW])
        sx = sb("sx", [P, BLOCKS, D])
        sxT = sb("sxT", [P, BLOCKS, P])
        w1_sb = sb("w1_sb", [P, RING, F])
        hid = sb("hid", [P, RING, FC, P])
        res = sb("res", [P, BLOCKS, D])

        ps = [stack.enter_context(nc.psum_tensor(f"ps{i}", [P, 512], F32)) for i in range(8)]

        x_in = [sem(f"x_in{h}") for h in range(NH)]
        c_in = [sem(f"c_in{h}") for h in range(NH)]
        kq_in, vcr_in, be_in, w2_in = sem("kq_in"), sem("vcr_in"), sem("be_in"), sem("w2_in")
        slots_cleared, slots_written = sem("slots_cleared"), sem("slots_written")
        rows_in = [sem(f"rows_in{g}") for g in range(G)]
        w1_in = [sem(f"w1_in{u}") for u in range(RING)]
        stored = sem("stored")
        diff_made, ident_made, masks_made, ones_made, norow_made, ids_made, iotas_made = (
            sem(n) for n in ("diff_made", "ident_made", "masks_made", "ones_made", "norow_made", "ids_made", "iotas_made"))
        half_made, eps_done, eps2_done = sem("half_made"), sem("eps_done"), sem("eps2_done")
        inv_done, row_made, bsel_done, gbc_done = sem("inv_done"), sem("row_made"), sem("bsel_done"), sem("gbc_done")
        share1_done, qk1_done = sem("share1_done"), sem("qk1_done")
        depth_made, earlier_made = sem("depth_made"), sem("earlier_made")
        (st_done, mv_done, rstd_done, xn_done, cT_ps, cT_done, xnT_ps, xnT_done, k_ps, q_ps, v_ps, sum_ps,
         k_act, q_act, kf_done, qf_done, share_done, qk_done, attn_done, tg_done, xb_done, y_ps, x1_done) = (
            sem(n) for n in ("st_done", "mv_done", "rstd_done", "xn_done", "cT_ps", "cT_done", "xnT_ps", "xnT_done",
                             "k_ps", "q_ps", "v_ps", "sum_ps", "k_act", "q_act", "kf_done", "qf_done",
                             "share_done", "qk_done", "attn_done", "tg_done", "xb_done", "y_ps", "x1_done"))
        (st2_done, mv2_done, rstd2_done, xn2_done, xn2T_ps, xn2T_done, logit_ps, logit_done, top_done, below_done,
         expo_done, total_done, pmax_done, gate_done, hit_done, score_done, best_done, onehot_done, count_ps,
         route_step, eb_done, place_done, pos_done) = (
            sem(n) for n in ("st2_done", "mv2_done", "rstd2_done", "xn2_done", "xn2T_ps", "xn2T_done", "logit_ps",
                             "logit_done", "top_done", "below_done", "expo_done", "total_done", "pmax_done",
                             "gate_done", "hit_done", "score_done", "best_done", "onehot_done", "count_ps",
                             "route_step", "eb_done", "place_done", "pos_done"))
        bsplit, sx_done, sxT_ps, sxT_done, h_ps, hid_done, e_ps, res_done = (
            sem(n) for n in ("bsplit", "sx_done", "sxT_ps", "sxT_done", "h_ps", "hid_done", "e_ps", "res_done"))

        block = stack.enter_context(nc.Block())

        @block.sync
        def _(sp):
            for h in range(NH):
                t = slice(h * TH, (h + 1) * TH)
                sp.dma_start(c_sb[:, t, :], ctx_rows[:, t, :]).then_inc(c_in[h], 16)
                sp.dma_start(x_sb[:, t, :], x_rows[:, t, :]).then_inc(x_in[h], 16)
            sp.dma_start(be_sb[:], expert_biases).then_inc(be_in, 16)
            sp.wait_ge(norow_made, 1)
            sp.dma_start(slots.rearrange("(p b) r -> p (b r)", p=P),
                         no_rows[:].bitcast(F32)).then_inc(slots_cleared, 16)
            sp.dma_start(w2_sb[:], w2.rearrange("e (c p) d -> p e c d", p=P)).then_inc(w2_in, 16)

            def load_w1(b, u, used):
                e = sp.value_load(eb[0:1, bass.ds(b, 1)], min_val=0, max_val=E - 1)
                if used is not None:
                    sp.wait_ge(h_ps, used)
                sp.dma_start(w1_sb[:, u, :], w1[bass.ds(e, 1), :, :].rearrange("o d f -> d (o f)")).then_inc(w1_in[u], 16)

            sp.wait_ge(eb_done, 1)
            for u in range(RING):
                load_w1(u, u, None)
            sp.wait_ge(slots_written, 16 * NT)
            for g in range(G):
                a, z = g * RING, (g + 1) * RING
                sp.dma_start(slot_rows[:, a:z, :],
                             slots[a * P:z * P, :].rearrange("(b p) r -> p b r", p=P)).then_inc(rows_in[g], 16)
            with sp.Fori(1, G) as i:
                for u in range(RING):
                    load_w1(RING * i + u, u, RING * i + u - (RING - 1))

        @block.gpsimd
        def _(pool):
            pool.iota(diff[:], [[1, P]], base=P, channel_multiplier=-1,
                      allow_small_or_imprecise_dtypes=True).then_inc(diff_made, 1)
            pool.memset(minus_half[:], -0.5).then_inc(half_made, 1)
            pool.memset(no_rows[:], NO_TOKEN).then_inc(norow_made, 1)
            pool.memset(ones[:], 1.0).then_inc(ones_made, 1)
            pool.iota(rows[:, :, ID].bitcast(I32), [[P, NT]], base=0, channel_multiplier=1).then_inc(ids_made, 1)

            def rstd(h, var, var_done, eps_done, done):
                pool.wait_ge(var_done, (h + 1) * TH)
                pool.tensor_scalar(var, var, EPS, None, ALU.add).then_inc(eps_done, 1)
                pool.wait_ge(eps_done, h + 1)
                pool.tensor_tensor(var, var, minus_half[:], ALU.pow).then_inc(done, 1)

            pool.wait_ge(half_made, 1)
            for h in range(NH):
                rstd(h, mv[:, h * TH:(h + 1) * TH, 1], mv_done, eps_done, rstd_done)
            pool.iota(rev[:], [[-1, E]], base=E, channel_multiplier=0,
                      allow_small_or_imprecise_dtypes=True).then_inc(iotas_made, 1)
            pool.iota(ediff[:], [[1, E], [-1, E]], base=0, channel_multiplier=0,
                      allow_small_or_imprecise_dtypes=True).then_inc(iotas_made, 1)
            pool.iota(first_slot[:], [[P, BLOCKS]], base=0, channel_multiplier=0,
                      allow_small_or_imprecise_dtypes=True).then_inc(iotas_made, 1)
            pool.iota(row_no[:], [[0, 1]], base=0, channel_multiplier=1).then_inc(iotas_made, 1)
            pool.wait_ge(vcr_in, 16)
            pool.wait_ge(tg_done, 1)
            pool.tensor_scalar(gated_bc[:], bc_sb, tg[:, 0:1], None, ALU.mult).then_inc(gbc_done, 1)
            pool.wait_ge(gbc_done, 1)
            for h in range(NH):
                ts = slice(h * TH, (h + 1) * TH)
                pool.tensor_tensor(xb[:, ts, :], x_sb[:, ts, :], gated_bc[:].unsqueeze(1).broadcast_to([P, TH, D]),
                                   ALU.add).then_inc(xb_done, 1)
            s = slice(0, W)
            pool.wait_ge(inv_done, 1)
            pool.tensor_tensor(share[:, s], kf[:, s], inv[:, s], ALU.mult).then_inc(share_done, 1)
            pool.wait_ge(share_done, 1)
            pool.wait_ge(qf_done, 1)
            pool.tensor_tensor(qk[:, s], qf[:, s], share[:, s], ALU.mult).then_inc(qk_done, 1)
            pool.wait_ge(be_in, 16)
            pool.tensor_copy(b_parts[:], be_sb[:]).then_inc(bsplit, 1)
            pool.wait_ge(bsplit, 1)
            pool.tensor_tensor(b_rest[:], be_sb[:], b_parts[:], ALU.subtract).then_inc(bsplit, 1)
            pool.wait_ge(bsplit, 2)
            pool.tensor_copy(b_mid[:], b_rest[:]).then_inc(bsplit, 1)
            pool.wait_ge(bsplit, 3)
            pool.tensor_copy(b_parts[BP:2 * BP, :], b_mid[BP:2 * BP, :]).then_inc(bsplit, 1)
            pool.wait_ge(bsplit, 4)
            pool.tensor_tensor(b_parts[2 * BP:BROWS, :], b_rest[2 * BP:BROWS, :], b_mid[2 * BP:BROWS, :],
                               ALU.subtract).then_inc(bsplit, 1)
            pool.wait_ge(bsplit, 5)
            for h in range(NH):
                rstd(h, rows[:, h * TH:(h + 1) * TH, RS], mv2_done, eps2_done, rstd2_done)
            pool.wait_ge(slots_cleared, 16)
            pool.wait_ge(ids_made, 1)
            pool.wait_ge(gate_done, 1)
            pool.wait_ge(pos_done, 1)
            for t in range(NT):
                pool.indirect_dma_start(
                    out=slots, out_offset=bass.IndirectOffsetOnAxis(ap=pos[:, t:t + 1].bitcast(U32), axis=0),
                    in_=rows[:, t, :], in_offset=None).then_inc(slots_written, 16)
            for b in range(BLOCKS):
                pool.wait_ge(res_done, b + 1)
                pool.indirect_dma_start(
                    out=out_rows,
                    out_offset=bass.IndirectOffsetOnAxis(ap=slot_rows[:, b, ID:ID + 1].bitcast(U32), axis=0),
                    in_=res[:, b, :], in_offset=None, bounds_check=T - 1, oob_is_err=False).then_inc(stored, 16)
            pool.wait_ge(stored, 16 * BLOCKS)

        @block.scalar
        def _(act):
            act.dma_start(kq_sb[:], kq_params).then_inc(kq_in, 16)
            act.dma_start(vcr_sb[:], vcr_params).then_inc(vcr_in, 16)

            def copy_ct(h):
                act.wait_ge(cT_ps, h + 1)
                act.activation(cT[:, h * W:(h + 1) * W], ps[4 * h][:], ACT.Copy).then_inc(cT_done, 1)

            def elu_parts(h, ready, bank, exp, relu, bias, done):
                s = slice(h * W, (h + 1) * W)
                act.wait_ge(ready, h + 1)
                act.activation(exp[:, s], bank[:], ACT.Exp, bias=bias).then_inc(done, 1)
                act.activation(relu[:, s], bank[:], ACT.Relu, bias=bias).then_inc(done, 1)

            def copy_xnt(h):
                act.wait_ge(xnT_ps, h + 1)
                act.activation(xnT[:, h * W:(h + 1) * W], ps[4 * h + 1][:], ACT.Copy).then_inc(xnT_done, 1)

            act.wait_ge(kq_in, 16)
            act.activation(tg[:], g_sb, ACT.Tanh).then_inc(tg_done, 1)
            copy_ct(0)
            copy_ct(1)
            elu_parts(0, k_ps, ps[2], kexp, krelu, bk_sb, k_act)
            copy_xnt(0)
            elu_parts(1, k_ps, ps[6], kexp, krelu, bk_sb, k_act)
            copy_xnt(1)
            elu_parts(0, q_ps, ps[3], qexp, qrelu, bq_sb, q_act)
            elu_parts(1, q_ps, ps[7], qexp, qrelu, bq_sb, q_act)
            for h in range(NH):
                s = slice(h * W, (h + 1) * W)
                act.wait_ge(xn2T_ps, h + 1)
                act.activation(xn2T[:, s], ps[4 * h + 3][:], ACT.Copy).then_inc(xn2T_done, 1)
            act.wait_ge(below_done, 1)
            act.activation(expo[:], below[:], ACT.Exp).then_inc(expo_done, 1)

            def copy_sxt(g):
                act.wait_ge(sxT_ps, g + 1)
                act.activation(sxT[:, g * RING:(g + 1) * RING, :],
                               ps[6 + g % 2][:, 0:RING * P].rearrange("p (b s) -> p b s", s=P),
                               ACT.Copy).then_inc(sxT_done, 1)

            def gelu(b, u, read):
                act.wait_ge(h_ps, b + 1)
                if read is not None:
                    act.wait_ge(e_ps, read)
                act.activation(hid[:, u, :, :], ps[u][:].rearrange("p (c s) -> p c s", c=FC),
                               ACT.Gelu).then_inc(hid_done, 1)

            copy_sxt(0)
            copy_sxt(1)
            for u in range(RING):
                gelu(u, u, None)
                copy_sxt(u + 2)
            with act.Fori(1, G) as i:
                for u in range(RING):
                    gelu(RING * i + u, u, RING * i + u - (RING - 1))

        @block.vector
        def _(dve):
            dve.wait_ge(diff_made, 1)
            dve.tensor_scalar(ident[:], diff[:], float(P), None, ALU.is_equal).then_inc(ident_made, 1)
            dve.tensor_copy(diff_i[:], diff[:]).then_inc(depth_made, 1)
            dve.tensor_scalar(before[:], diff[:], float(P), None, ALU.is_gt).then_inc(masks_made, 1)
            dve.wait_ge(depth_made, 1)
            dve.tensor_scalar(depth_diff[:], diff_i[:], D // HEADS - 1, None, ALU.bitwise_and).then_inc(depth_made, 1)
            dve.wait_ge(depth_made, 2)
            dve.tensor_scalar(same_depth[:], depth_diff[:], 0.0, None, ALU.is_equal).then_inc(depth_made, 1)
            dve.wait_ge(depth_made, 3)
            dve.scalar_tensor_tensor(head_sum[:], diff[:], float(P), same_depth[:], ALU.is_ge, ALU.mult).then_inc(masks_made, 1)

            def mean_var(h, src, stats, pair, st_done, mv_done):
                for t in range(h * TH, (h + 1) * TH):
                    dve.bn_stats(stats[:, t, :], src[:, t, 0:D]).then_inc(st_done, 1)
                for t in range(h * TH, (h + 1) * TH):
                    dve.wait_ge(st_done, t + 1)
                    dve.bn_aggr(pair[:, t, :], stats[:, t, :]).then_inc(mv_done, 1)

            def normalise(h, src, pair, dst, rstd_done, done):
                dve.wait_ge(rstd_done, h + 1)
                for t in range(h * TH, (h + 1) * TH):
                    last = dve.tensor_scalar(dst[:, t, :], src[:, t, 0:D], pair[:, t, 0:1], pair[:, t, 1:2],
                                             ALU.subtract, ALU.mult)
                last.then_inc(done, 1)

            for h in range(NH):
                dve.wait_ge(x_in[h], 16)
                mean_var(h, x_sb, stats, mv, st_done, mv_done)
            normalise(0, x_sb, mv, xn, rstd_done, xn_done)
            normalise(1, x_sb, mv, xn, rstd_done, xn_done)

            def elu_sum(dst, exp, relu, h, arrived, done):
                s = slice(h * W, (h + 1) * W)
                dve.wait_ge(arrived, 2 * h + 2)
                dve.scalar_tensor_tensor(dst[:, s], exp[:, s], 1.0, relu[:, s], ALU.min, ALU.add).then_inc(done, 1)

            elu_sum(kf, kexp, krelu, 0, k_act, kf_done)
            elu_sum(kf, kexp, krelu, 1, k_act, kf_done)
            for h in range(NH):
                dve.wait_ge(sum_ps, h + 1)
                dve.reciprocal(inv[:, h * W:(h + 1) * W], ps[4 * h][:]).then_inc(inv_done, 1)
                elu_sum(qf, qexp, qrelu, h, q_act, qf_done)
            dve.wait_ge(iotas_made, 4)
            dve.tensor_scalar(earlier[:], ediff[:], 0.0, None, ALU.is_gt).then_inc(earlier_made, 1)
            dve.tensor_scalar(row_low[:], row_no[:], E - 1, None, ALU.bitwise_and).then_inc(row_made, 1)
            dve.wait_ge(row_made, 1)
            dve.tensor_copy(row_e[:], row_low[:]).then_inc(row_made, 1)
            s = slice(W, T)
            dve.wait_ge(inv_done, 2)
            dve.tensor_tensor(share[:, s], kf[:, s], inv[:, s], ALU.mult).then_inc(share1_done, 1)
            dve.wait_ge(share1_done, 1)
            dve.wait_ge(qf_done, 2)
            dve.tensor_tensor(qk[:, s], qf[:, s], share[:, s], ALU.mult).then_inc(qk1_done, 1)
            for h, ready in enumerate((qk_done, qk1_done)):
                s = slice(h * W, (h + 1) * W)
                dve.wait_ge(v_ps, h + 1)
                dve.wait_ge(ready, 1)
                dve.scalar_tensor_tensor(attn[:, s], ps[4 * h + 1][:], bv_sb, qk[:, s], ALU.add, ALU.mult).then_inc(attn_done, 1)
            pair2 = rows[:, :, MU:MU + 2]
            for h in range(NH):
                ts = slice(h * TH, (h + 1) * TH)
                dve.wait_ge(y_ps, h + 1)
                dve.wait_ge(xb_done, h + 1)
                dve.scalar_tensor_tensor(rows[:, ts, 0:D], ps[4 * h + 2][:].rearrange("p (t d) -> p t d", d=D), tg[:, 0:1],
                                         xb[:, ts, :], ALU.mult, ALU.add).then_inc(x1_done, 1)
                dve.wait_ge(x1_done, h + 1)
                mean_var(h, rows, stats2, pair2, st2_done, mv2_done)
            for h in range(NH):
                normalise(h, rows, pair2, xn2, rstd2_done, xn2_done)

            te = [P, NT, E]
            for h in range(NH):
                dve.wait_ge(logit_ps, h + 1)
                dve.tensor_copy(logit[:, h * TH:(h + 1) * TH, :],
                                ps[4 * h][:, 0:TH * E].rearrange("p (t e) -> p t e", e=E)).then_inc(logit_done, 1)
            dve.wait_ge(logit_done, NH)
            dve.reduce_max(top[:], logit[:], AX_X).then_inc(top_done, 1)
            dve.wait_ge(top_done, 1)
            dve.tensor_tensor(hit[:], logit[:], top[:].unsqueeze(2).broadcast_to(te), ALU.is_equal).then_inc(hit_done, 1)
            dve.tensor_tensor(below[:], logit[:], top[:].unsqueeze(2).broadcast_to(te), ALU.subtract).then_inc(below_done, 1)
            dve.wait_ge(hit_done, 1)
            dve.tensor_tensor(score[:], hit[:], rev[:].unsqueeze(1).broadcast_to(te), ALU.mult).then_inc(score_done, 1)
            dve.wait_ge(score_done, 1)
            dve.reduce_max(best[:], score[:], AX_X).then_inc(best_done, 1)
            dve.wait_ge(best_done, 1)
            dve.tensor_tensor(onehot[:], score[:], best[:].unsqueeze(2).broadcast_to(te), ALU.is_equal).then_inc(onehot_done, 1)
            dve.wait_ge(expo_done, 1)
            dve.reduce_sum(total[:], expo[:], AX_X).then_inc(total_done, 1)
            dve.wait_ge(total_done, 1)
            dve.reciprocal(pmax[:], total[:]).then_inc(pmax_done, 1)
            dve.wait_ge(pmax_done, 1)
            dve.tensor_scalar(rows[:, :, GATE], pmax[:], tg[:, 1:2], None, ALU.mult).then_inc(gate_done, 1)
            rank, many = ps[1][:, 0:NT * E], ps[1][:, NT * E:NT * E + E]
            dve.wait_ge(count_ps, 1)
            dve.tensor_scalar(padded[:], many, float(P - 1), None, ALU.add).then_inc(route_step, 1)
            dve.wait_ge(route_step, 1)
            dve.tensor_scalar(room[:], padded[:], 7, 7, ALU.logical_shift_right, ALU.logical_shift_left).then_inc(route_step, 1)
            dve.wait_ge(route_step, 2)
            dve.wait_ge(earlier_made, 1)
            dve.tensor_tensor(eprod[:], earlier[:], room[:].unsqueeze(1).broadcast_to([P, E, E]), ALU.mult).then_inc(route_step, 1)
            dve.wait_ge(route_step, 3)
            dve.reduce_sum(base[:], eprod[:], AX_X).then_inc(route_step, 1)
            dve.wait_ge(route_step, 4)
            dve.tensor_tensor(place[:], rank.rearrange("p (t e) -> p t e", e=E),
                              base[:].unsqueeze(1).broadcast_to(te), ALU.add).then_inc(route_step, 1)
            dve.wait_ge(route_step, 5)
            dve.tensor_tensor(placed[:], place[:], onehot[:], ALU.mult).then_inc(route_step, 1)
            dve.wait_ge(route_step, 6)
            dve.reduce_sum(pos_f[:], placed[:], AX_X).then_inc(route_step, 1)
            dve.wait_ge(route_step, 7)
            dve.tensor_copy(pos[:], pos_f[:]).then_inc(pos_done, 1)
            be = [P, BLOCKS, E]
            dve.tensor_tensor(stop_of[:], base[:], room[:], ALU.add).then_inc(route_step, 1)
            dve.wait_ge(route_step, 8)
            dve.tensor_tensor(passed[:], stop_of[:].unsqueeze(1).broadcast_to(be),
                              first_slot[:].unsqueeze(2).broadcast_to(be), ALU.is_le).then_inc(route_step, 1)
            dve.wait_ge(route_step, 9)
            dve.reduce_sum(eb_f[:], passed[:], AX_X).then_inc(route_step, 1)
            dve.wait_ge(route_step, 10)
            dve.tensor_scalar(eb[:], eb_f[0:1, :], float(E - 1), None, ALU.min).then_inc(eb_done, 1)
            dve.wait_ge(row_made, 2)
            dve.tensor_scalar(b_select[:], eb_f[0:BROWS, :], row_e[:], None, ALU.is_equal).then_inc(bsel_done, 1)

            for g in range(G):
                dve.wait_ge(rows_in[g], 16)
                for b in range(g * RING, (g + 1) * RING):
                    last = dve.tensor_scalar(sx[:, b, :], slot_rows[:, b, 0:D], slot_rows[:, b, MU:MU + 1],
                                             slot_rows[:, b, RS:RS + 1], ALU.subtract, ALU.mult)
                last.then_inc(sx_done, 1)

            with dve.Fori(0, G) as i:
                for u in range(RING):
                    b = RING * i + u
                    dve.wait_ge(e_ps, b + 1)
                    dve.scalar_tensor_tensor(res[:, bass.ds(b, 1), :].rearrange("p o d -> p (o d)"), ps[3 + u][:, 0:D],
                                             slot_rows[:, bass.ds(b, 1), GATE],
                                             slot_rows[:, bass.ds(b, 1), 0:D].rearrange("p o d -> p (o d)"),
                                             ALU.mult, ALU.add).then_inc(res_done, 1)

        @block.tensor
        def _(pe):
            def turn(dst, src):
                return pe.transpose(dst, src, ident[:])

            pe.wait_ge(ident_made, 1)
            for h in range(NH):
                pe.wait_ge(c_in[h], 16)
                for t in range(TH):
                    mm = turn(ps[4 * h][:, t * P:(t + 1) * P], c_sb[:, h * TH + t, :])
                mm.then_inc(cT_ps, 1)
            pe.wait_ge(kq_in, 16)

            def turn_xn(h):
                pe.wait_ge(xn_done, h + 1)
                for t in range(TH):
                    mm = turn(ps[4 * h + 1][:, t * P:(t + 1) * P], xn[:, h * TH + t, :])
                mm.then_inc(xnT_ps, 1)

            def keys(h):
                pe.wait_ge(cT_done, h + 1)
                pe.matmul(ps[4 * h + 2][:], wk_sb, cT[:, h * W:(h + 1) * W], start=True, stop=True).then_inc(k_ps, 1)

            def queries(h):
                pe.wait_ge(xnT_done, h + 1)
                pe.matmul(ps[4 * h + 3][:], wq_sb, xnT[:, h * W:(h + 1) * W], start=True, stop=True).then_inc(q_ps, 1)

            def sums(h):
                pe.wait_ge(kf_done, h + 1)
                pe.matmul(ps[4 * h][:], head_sum[:], kf[:, h * W:(h + 1) * W], start=True, stop=True).then_inc(sum_ps, 1)

            def values(h):
                pe.matmul(ps[4 * h + 1][:], wv_sb, cT[:, h * W:(h + 1) * W], start=True, stop=True).then_inc(v_ps, 1)

            keys(0)
            turn_xn(0)
            keys(1)
            pe.wait_ge(masks_made, 2)
            sums(0)
            turn_xn(1)
            queries(0)
            sums(1)
            queries(1)
            pe.wait_ge(vcr_in, 16)
            values(0)
            values(1)
            for h in range(NH):
                pe.wait_ge(attn_done, h + 1)
                for t in range(TH):
                    mm = pe.matmul(ps[4 * h + 2][:, t * P:(t + 1) * P], attn[:, (h * TH + t) * P:(h * TH + t + 1) * P],
                                   wc_sb, start=True, stop=True)
                mm.then_inc(y_ps, 1)
            for h in range(NH):
                pe.wait_ge(xn2_done, h + 1)
                for t in range(TH):
                    mm = turn(ps[4 * h + 3][:, t * P:(t + 1) * P], xn2[:, h * TH + t, :])
                mm.then_inc(xn2T_ps, 1)
            for h in range(NH):
                pe.wait_ge(xn2T_done, h + 1)
                for t in range(TH):
                    mm = pe.matmul(ps[4 * h][:, t * E:(t + 1) * E], xn2T[:, (h * TH + t) * P:(h * TH + t + 1) * P],
                                   wr_sb, start=True, stop=True)
                mm.then_inc(logit_ps, 1)
            pe.wait_ge(ones_made, 1)
            pe.wait_ge(onehot_done, 1)
            R = ps[1]
            pe.matmul(R[:, 0:NT * E], before[:], onehot[:], start=True, stop=True)
            for t in range(NT - 1):
                later = NT - 1 - t
                pe.matmul(R[:, (t + 1) * E:NT * E].rearrange("p (t e) -> p t e", e=E), ones[:],
                          onehot[:, t:t + 1, :].broadcast_to([P, later, E]),
                          start=False, stop=True, skip_group_check=True)
            for t in range(NT):
                mm = pe.matmul(R[:, NT * E:NT * E + E], ones[:], onehot[:, t, :], start=(t == 0), stop=(t == NT - 1))
            mm.then_inc(count_ps, 1)

            def turn_sx(g):
                pe.wait_ge(sx_done, g + 1)
                if g >= 2:
                    pe.wait_ge(sxT_done, g - 1)
                for j in range(RING):
                    mm = turn(ps[6 + g % 2][:, j * P:(j + 1) * P], sx[:, g * RING + j, :])
                mm.then_inc(sxT_ps, 1)

            def hidden(b, u, nth):
                pe.wait_ge(w1_in[u], 16 * nth)
                for c in range(FC):
                    to = ps[u][:, c * P:(c + 1) * P]
                    pe.matmul(to, b_parts[:, c * P:(c + 1) * P], b_select[:, bass.ds(b, 1)].broadcast_to([BROWS, P]),
                              start=True, stop=False)
                    mm = pe.matmul(to, w1_sb[:, u, c * P:(c + 1) * P],
                                   sxT[:, bass.ds(b, 1), :].rearrange("p o s -> p (o s)"), start=False, stop=True)
                mm.then_inc(h_ps, 1)

            def expert(b):
                return pe.value_load(eb[0:1, bass.ds(b, 1)], min_val=0, max_val=E - 1)

            def result(b, u, e, read):
                to = ps[3 + u][:, 0:D]
                if read is not None:
                    pe.wait_ge(res_done, read)
                pe.matmul(to, b_select[:, bass.ds(b, 1)].broadcast_to([BROWS, P]), b_parts[:, F:NB],
                          start=True, stop=False)
                pe.wait_ge(hid_done, b + 1)
                for c in range(FC):
                    mm = pe.matmul(to, hid[:, u, c, :], w2_sb[:, bass.ds(e, 1), c, :].rearrange("p o d -> p (o d)"),
                                   start=False, stop=(c == FC - 1))
                mm.then_inc(e_ps, 1)

            pe.wait_ge(eb_done, 1)
            pe.wait_ge(bsel_done, 1)
            pe.wait_ge(bsplit, 5)
            pe.wait_ge(w2_in, 16)
            turn_sx(0)
            turn_sx(1)
            pe.wait_ge(sxT_done, 1)
            hidden(0, 0, 1)
            for b in range(RING):
                e = expert(b)
                if b == RING - 1:
                    pe.wait_ge(sxT_done, 2)
                hidden(b + 1, (b + 1) % RING, (b + 1) // RING + 1)
                result(b, b, e, None)
                turn_sx(b + 2)
            pe.wait_ge(sxT_done, G)
            with pe.Fori(1, G - 1) as i:
                for u in range(RING):
                    b = RING * i + u
                    e = expert(b)
                    hidden(b + 1, (u + 1) % RING, i + 1 + (u + 1) // RING)
                    result(b, u, e, b - (RING - 1))
            for b in range(BLOCKS - RING, BLOCKS):
                e = expert(b)
                if b + 1 < BLOCKS:
                    hidden(b + 1, (b + 1) % RING, G)
                result(b, b % RING, e, b - (RING - 1))


_OUTS = [((8, 128, 128), 'float32')]


def kernel(**inputs):
    import numpy as _np
    import concourse.bacc as _bacc
    from concourse import mybir as _mybir
    from concourse.bass_utils import run_bass_kernel_spmd as _run

    a = {name: _np.asarray(value) for name, value in inputs.items()}
    P = 128

    def rows(v):
        return _np.broadcast_to(v, (P, v.shape[-1]))

    def column(v):
        return v.reshape(P, 1)

    biases = _np.concatenate([a['L0_ffn_b1'], a['L0_ffn_b2']], axis=1)
    spaced = _np.zeros((72, biases.shape[1]), biases.dtype)
    for part in range(3):
        spaced[32 * part:32 * part + 8] = biases
    laid = {
        'x': a['x'],
        'ctx': a['ctx_1024'],
        'kq_params': _np.concatenate([a['L0_xattn_wk_w'], a['L0_xattn_wq_w'], column(a['L0_xattn_wk_b']),
                                      column(a['L0_xattn_wq_b']), rows(a['g_xattn']), rows(a['g_ffn'])], axis=1),
        'vcr_params': _np.concatenate([a['L0_xattn_wv_w'], a['L0_xattn_wc_w'], a['L0_ffn_Wr'],
                                       column(a['L0_xattn_wv_b']), rows(a['L0_xattn_wc_b'])], axis=1),
        'expert_biases': spaced,
        'w1': a['L0_ffn_W1'],
        'w2': a['L0_ffn_W2'],
    }
    nc = _bacc.Bacc("TRN2", target_bir_lowering=False, num_devices=1)
    arrays, args = {}, []
    for name, value in laid.items():
        value = _np.ascontiguousarray(value)
        arrays[f"in_{name}_dram"] = value
        args.append(nc.dram_tensor(f"in_{name}_dram", value.shape, _mybir.dt.from_np(value.dtype),
                                   kind="ExternalInput").ap())
    for i, (shape, dtype) in enumerate(_OUTS):
        dt = _mybir.dt.from_np(_np.dtype(dtype))
        args.append(nc.dram_tensor(f"out_{i}_dram", shape, dt, kind="ExternalOutput").ap())
    gated_block_kernel(nc, *args)
    r = _run(nc, [arrays], core_ids=[0])
    return r.results[0]["out_0_dram"]
```

```python
from contextlib import ExitStack

import concourse.bass as bass
from concourse import mybir

ALU = mybir.AluOpType
ACT = mybir.ActivationFunctionType
F32 = mybir.dt.float32
BF16 = mybir.dt.bfloat16
I32 = mybir.dt.int32
U32 = mybir.dt.uint32
AX_X = mybir.AxisListType.X

P = 128
HEADS = 16
EPS = 1e-5
NO_TOKEN = 65535


def gated_block_kernel(nc, x, ctx, kq_params, vcr_params, w1, w2, b2, out):
    B, S, D = x.shape
    E, _, F = w1.shape
    T = B * S
    NT = T // P
    NH = 2
    TH = NT // NH
    W = TH * P
    FC = F // P
    BLOCKS = (T + E * (P - 1)) // P
    RING = 3
    G = BLOCKS // RING
    EARLY = 2
    PACKS = [(0, 1), (1, 2), (2, 3), (3, 4), (4, 6), (6, 8), (8, 10), (10, 12), (12, 15)]
    WARM, WARM_START = 4, 7
    BY_SYNC, BY_SCALAR = range(EARLY, 8), range(8, 10)
    MU, RS, GATE, ID, ROW = D, D + 1, D + 2, D + 3, D + 4
    assert PACKS[-1][1] == BLOCKS and len(PACKS) == 2 * RING + 3
    assert S == P and D == P and W == 512 and F == 512 and BLOCKS == G * RING and E == 8

    x_rows = x.rearrange("b p d -> p b d")
    ctx_rows = ctx.rearrange("b p d -> p b d")
    out_rows = out.rearrange("b p d -> (b p) d")
    NONE = E * T
    SLOTS = NONE + P
    COPIES = 5
    assert SLOTS % (P * COPIES) == 0
    slots = nc.dram_tensor("slots", (SLOTS, ROW), F32).ap()

    with ExitStack() as stack:
        def sb(name, shape, dt=F32):
            return stack.enter_context(nc.sbuf_tensor(name, shape, dt))

        def sem(name):
            return stack.enter_context(nc.semaphore(name))

        x_sb = sb("x_sb", [P, NT, D])
        c_sb = sb("c_sb", [P, NT, D])
        kq_sb = sb("kq_sb", [P, 2 * D + 4])
        wk_sb, wq_sb = kq_sb[:, 0:D], kq_sb[:, D:2 * D]
        bk_sb, bq_sb, g_sb = kq_sb[:, 2 * D:2 * D + 1], kq_sb[:, 2 * D + 1:2 * D + 2], kq_sb[:, 2 * D + 2:2 * D + 4]
        vcr_sb = sb("vcr_sb", [P, 3 * D + E + 1 + E * FC])
        wv_sb, wc_sb, wr_sb = vcr_sb[:, 0:D], vcr_sb[:, D:2 * D], vcr_sb[:, 2 * D:2 * D + E]
        bv_sb, bc_sb = vcr_sb[:, 2 * D + E:2 * D + E + 1], vcr_sb[:, 2 * D + E + 1:3 * D + E + 1]
        b1_sb = vcr_sb[:, 3 * D + E + 1:].rearrange("p (e c) -> p e c", c=FC)
        b2_sb = sb("b2_sb", [P, E, D])
        w2_sb = [sb(f"w2_sb{c}", [P, E, D]) for c in range(FC)]
        diff = sb("diff", [P, P])
        ident = sb("ident", [P, P])
        diff_i = sb("diff_i", [P, P], I32)
        centre = sb("centre", [P, P])
        depth_diff = sb("depth_diff", [P, P], I32)
        same_depth = sb("same_depth", [P, P])
        minus_half = sb("minus_half", [P, TH])
        head_sum = sb("head_sum", [P, P])
        before = sb("before", [P, P], BF16)
        ones = sb("ones", [P, P], BF16)
        rev = sb("rev", [P, E])
        ediff = sb("ediff", [P, E, E])
        not_later = sb("not_later", [P, E, E])
        first_slot = sb("first_slot", [P, BLOCKS])
        expert_slot = sb("expert_slot", [1, TH, E], BF16)
        no_rows = sb("no_rows", [P, SLOTS // P // COPIES * ROW], U32)
        stats = sb("stats", [P, NT, 6])
        mv = sb("mv", [P, NT, 2])
        xn = sb("xn", [P, NT, D])
        tg = sb("tg", [P, 2])
        xb = sb("xb", [P, NT, D])
        cT, xnT, kexp, krelu, qexp, qrelu, kf, qf, inv, v, vk, vqk, attn = (
            sb(n, [P, T]) for n in "cT xnT kexp krelu qexp qrelu kf qf inv v vk vqk attn".split())
        gated_bc = sb("gated_bc", [P, D])
        rows = sb("rows", [P, NT, ROW])
        stats2 = sb("stats2", [P, NT, 6])
        x1T = sb("x1T", [P, T])
        minus_mu = sb("minus_mu", [P, NT])
        xn2 = sb("xn2", [P, NT, D])
        slot_no = sb("slot_no", [P, P])
        slot_in = sb("slot_in", [P, EARLY, NT])
        select = sb("select", [P, EARLY, NT, P])
        wr_centred = sb("wr_centred", [P, E])
        below_scaled = sb("below_scaled", [P, NT, E])
        top = sb("top", [P, NT])
        below = sb("below", [P, NT, E])
        expo = sb("expo", [P, NT, E])
        total = sb("total", [P, NT])
        pmax = sb("pmax", [P, NT])
        hit = sb("hit", [P, NT, E])
        score = sb("score", [P, NT, E])
        best = sb("best", [P, NT])
        onehot = sb("onehot", [P, NT, E], BF16)
        padded = sb("padded", [P, E], I32)
        room = sb("room", [P, E], I32)
        eprod = sb("eprod", [P, E, E])
        stop_of = sb("stop_of", [P, E])
        passed = sb("passed", [P, BLOCKS, E])
        eb_f = sb("eb_f", [P, BLOCKS])
        eb = sb("eb", [1, BLOCKS], I32)
        placed = sb("placed", [P, NT, E])
        pos_f = sb("pos_f", [P, NT])
        room_before = sb("room_before", [P, BLOCKS, E])
        used_before = sb("used_before", [P, BLOCKS])
        slot_sum = sb("slot_sum", [P, BLOCKS])
        start_f = sb("start_f", [P, BLOCKS])
        start = sb("start", [1, BLOCKS], I32)
        pos = sb("pos", [P, NT], I32)
        slot_rows = sb("slot_rows", [P, BLOCKS, ROW])
        sx = sb("sx", [P, BLOCKS, D])
        sxT = sb("sxT", [P, BLOCKS, P])
        w1_sb = sb("w1_sb", [P, RING, F])
        w1_early = sb("w1_early", [P, EARLY, F])
        hid = sb("hid", [P, RING, FC, P])
        gelu_warm = sb("gelu_warm", [P, 1])
        xb2 = sb("xb2", [P, BLOCKS, D])
        res = sb("res", [P, BLOCKS, D])

        ps = [stack.enter_context(nc.psum_tensor(f"ps{i}", [P, 512], F32)) for i in range(8)]

        def sems(names):
            return [sem(n) for n in names.split()]

        x_in = [sem(f"x_in{h}") for h in range(NH)]
        c_in = [sem(f"c_in{h}") for h in range(NH)]
        kq_in, vcr_in, b2_in, w2_in = sems("kq_in vcr_in b2_in w2_in")
        slots_cleared, slots_written = sems("slots_cleared slots_written")
        rows_in = [sem(f"rows_in{p}") for p in range(len(PACKS))]
        w1_early_in = [sem(f"w1_early_in{b}") for b in range(EARLY)]
        w1_in = [sem(f"w1_in{u}") for u in range(RING)]
        stored = sem("stored")
        diff_made, ident_made, centre_made, depth_made, masks_made, ones_made, half_made = sems(
            "diff_made ident_made centre_made depth_made masks_made ones_made half_made")
        norow_made, ids_made, iotas_made, eslot_made, not_later_made = sems(
            "norow_made ids_made iotas_made eslot_made not_later_made")
        wrc_ps, wrc_done = sems("wrc_ps wrc_done")
        st_done, mv_done, eps_done, rstd_done, xn_done = sems(
            "st_done mv_done eps_done rstd_done xn_done")
        cT_ps, cT_done, xnT_ps, xnT_done, k_ps, q_ps, v_ps, v_done, sum_ps = sems(
            "cT_ps cT_done xnT_ps xnT_done k_ps q_ps v_ps v_done sum_ps")
        k_act, q_act = sems("k_act q_act")
        kf_done, qf0_done, qf1_done, vk_done, vqk0_done, vqk1_done, inv_done, attn_done = sems(
            "kf_done qf0_done qf1_done vk_done vqk0_done vqk1_done inv_done attn_done")
        tg_done, gated_bc_done, xb_done, y_ps, x1_done = sems("tg_done gated_bc_done xb_done y_ps x1_done")
        st2_done, mv2_done, eps2_done, rstd2_done, minus_mu_done, xn2_done = sems(
            "st2_done mv2_done eps2_done rstd2_done minus_mu_done xn2_done")
        x1T_ps, x1T_done, logit_ps, top_done, hit_done, score_done, best_done, onehot_done = sems(
            "x1T_ps x1T_done logit_ps top_done hit_done score_done best_done onehot_done")
        below_done, scaled_done, expo_done, total_done, pmax_done, gate_done = sems(
            "below_done scaled_done expo_done total_done pmax_done gate_done")
        rank_ps, placed_done, posf_done, pos_done = sems("rank_ps placed_done posf_done pos_done")
        count_ps, padded_done, room_done, eprod_done, stop_done, passed_done, ebf_done, eb_done = sems(
            "count_ps padded_done room_done eprod_done stop_done passed_done ebf_done eb_done")
        room_before_done, used_done, slot_sum_done, startf_done, start_done = sems(
            "room_before_done used_done slot_sum_done startf_done start_done")
        slot_in_done, select_done = sems("slot_in_done select_done")
        h_ps, hid_done, e_ps, xb2_done, res_done = sems("h_ps hid_done e_ps xb2_done res_done")
        sx_done, sxT_ps, sxT_done = sems("sx_done sxT_ps sxT_done")

        def pack_of(b):
            return next(p for p, (a, z) in enumerate(PACKS) if a <= b < z)

        def expert_of(engine, b):
            return engine.value_load(eb[0:1, bass.ds(b, 1)], min_val=0, max_val=E - 1)

        def load_w1(queue, b, to, arrived, used):
            e = expert_of(queue, b)
            if used is not None:
                queue.wait_ge(h_ps, used)
            queue.dma_start(to, w1[bass.ds(e, 1), :, :].rearrange("o d f -> d (o f)")).then_inc(arrived, 16)

        def first_slot_of(queue, b):
            return queue.value_load(start[0:1, b:b + 1], min_val=0, max_val=NONE)

        def load_rows(queue, b, first):
            queue.dma_start(slot_rows[:, b, :], slots[bass.ds(first, P), :]).then_inc(rows_in[pack_of(b)], 16)

        block = stack.enter_context(nc.Block())

        @block.sync
        def _(sp):
            for h in range(NH):
                t = slice(h * TH, (h + 1) * TH)
                sp.dma_start(c_sb[:, t, :], ctx_rows[:, t, :]).then_inc(c_in[h], 16)
                sp.dma_start(x_sb[:, t, :], x_rows[:, t, :]).then_inc(x_in[h], 16)
            sp.dma_start(vcr_sb[:], vcr_params).then_inc(vcr_in, 16)
            sp.wait_ge(norow_made, 1)
            sp.dma_start(slots.rearrange("(p c b) r -> p c (b r)", p=P, c=COPIES),
                         no_rows[:].bitcast(F32).unsqueeze(1).broadcast_to([P, COPIES, SLOTS // P // COPIES * ROW]))\
              .then_inc(slots_cleared, 16)
            for c in range(FC):
                sp.dma_start(w2_sb[c][:], w2[:, c * P:(c + 1) * P, :].rearrange("e p d -> p e d")).then_inc(w2_in, 16)
            sp.dma_start(b2_sb[:], b2.unsqueeze(0).broadcast_to([P, E, D])).then_inc(b2_in, 16)

            sp.wait_ge(eb_done, 1)
            for b in range(EARLY):
                load_w1(sp, b, w1_early[:, b, :], w1_early_in[b], None)
            load_w1(sp, EARLY, w1_sb[:, EARLY, :], w1_in[EARLY], None)

            sp.wait_ge(start_done, 1)
            _, firsts = nc.values_load_multi_w_load_instructions(
                start[0:1, BY_SYNC[0]:BY_SYNC[-1] + 1], engines=[mybir.EngineType.SP], min_val=0, max_val=NONE)
            sp.wait_ge(slots_written, 16 * NT)
            for b, first in zip(BY_SYNC, firsts):
                load_rows(sp, b, first)

            def load_w1_to_ring(b, u):
                load_w1(sp, b, w1_sb[:, u, :], w1_in[u], b - (RING - 1))

            for b in (2 * RING - 1, 2 * RING):
                load_w1_to_ring(b, b % RING)
            with sp.Fori(2, G - 1) as i:
                for u in range(1, RING + 1):
                    load_w1_to_ring(RING * i + u, u % RING)
            for b in range(BLOCKS - 2, BLOCKS):
                load_w1_to_ring(b, b % RING)

        @block.gpsimd
        def _(pool):
            pool.iota(diff[:], [[1, P]], base=P, channel_multiplier=-1,
                      allow_small_or_imprecise_dtypes=True).then_inc(diff_made, 1)
            pool.memset(minus_half[:], -0.5).then_inc(half_made, 1)
            pool.memset(no_rows[:], NO_TOKEN).then_inc(norow_made, 1)
            pool.iota(rows[:, :, ID].bitcast(I32), [[P, NT]], base=0, channel_multiplier=1).then_inc(ids_made, 1)

            def rstd(h, var, var_done, added, done):
                pool.wait_ge(var_done, (h + 1) * TH)
                pool.tensor_scalar(var, var, EPS, None, ALU.add).then_inc(added, 1)
                pool.wait_ge(added, h + 1)
                pool.tensor_tensor(var, var, minus_half[:], ALU.pow).then_inc(done, 1)

            pool.iota(rev[:], [[-1, E]], base=E, channel_multiplier=0,
                      allow_small_or_imprecise_dtypes=True).then_inc(iotas_made, 1)
            pool.iota(ediff[:], [[1, E], [-1, E]], base=0, channel_multiplier=0,
                      allow_small_or_imprecise_dtypes=True).then_inc(iotas_made, 1)
            pool.iota(first_slot[:], [[P, BLOCKS]], base=0, channel_multiplier=0,
                      allow_small_or_imprecise_dtypes=True).then_inc(iotas_made, 1)
            pool.iota(slot_no[:], [[1, P]], base=0, channel_multiplier=0,
                      allow_small_or_imprecise_dtypes=True).then_inc(iotas_made, 1)
            pool.iota(expert_slot[:], [[0, TH], [T, E]], base=0, channel_multiplier=0,
                      allow_small_or_imprecise_dtypes=True).then_inc(eslot_made, 1)
            pool.wait_ge(half_made, 1)
            for h in range(NH):
                rstd(h, mv[:, h * TH:(h + 1) * TH, 1], mv_done, eps_done, rstd_done)

            def v_times_k(h):
                s = slice(h * W, (h + 1) * W)
                pool.wait_ge(v_done, h + 1)
                pool.wait_ge(kf_done, h + 1)
                pool.tensor_tensor(vk[:, s], v[:, s], kf[:, s], ALU.mult).then_inc(vk_done, 1)

            def residual_base(h):
                ts = slice(h * TH, (h + 1) * TH)
                pool.tensor_tensor(xb[:, ts, :], x_sb[:, ts, :], gated_bc[:].unsqueeze(1).broadcast_to([P, TH, D]),
                                   ALU.add).then_inc(xb_done, 1)

            v_times_k(0)
            pool.wait_ge(tg_done, 1)
            pool.tensor_scalar(gated_bc[:], bc_sb, tg[:, 0:1], None, ALU.mult).then_inc(gated_bc_done, 1)
            pool.wait_ge(gated_bc_done, 1)
            residual_base(0)
            v_times_k(1)
            s = slice(0, W)
            pool.wait_ge(vk_done, 1)
            pool.wait_ge(qf0_done, 1)
            pool.tensor_tensor(vqk[:, s], vk[:, s], qf[:, s], ALU.mult).then_inc(vqk0_done, 1)
            residual_base(1)
            for h in range(NH):
                rstd(h, rows[:, h * TH:(h + 1) * TH, RS], mv2_done, eps2_done, rstd2_done)
            pool.wait_ge(slots_cleared, 16)
            pool.wait_ge(ids_made, 1)
            for t in range(NT):
                if t % TH == 0:
                    pool.wait_ge(gate_done, t // TH + 1)
                    pool.wait_ge(pos_done, t // TH + 1)
                pool.indirect_dma_start(
                    out=slots, out_offset=bass.IndirectOffsetOnAxis(ap=pos[:, t:t + 1].bitcast(U32), axis=0),
                    in_=rows[:, t, :], in_offset=None).then_inc(slots_written, 16)
            pool.wait_ge(start_done, 1)
            pool.wait_ge(slots_written, 16 * NT)
            for b in [b for b in range(BLOCKS) if b not in BY_SYNC and b not in BY_SCALAR]:
                load_rows(pool, b, first_slot_of(pool, b))
            for b in range(BLOCKS):
                pool.wait_ge(res_done, b + 1)
                pool.indirect_dma_start(
                    out=out_rows,
                    out_offset=bass.IndirectOffsetOnAxis(ap=slot_rows[:, b, ID:ID + 1].bitcast(U32), axis=0),
                    in_=res[:, b, :], in_offset=None, bounds_check=T - 1, oob_is_err=False).then_inc(stored, 16)
            pool.wait_ge(stored, 16 * BLOCKS)

        @block.scalar
        def _(act):
            act.dma_start(kq_sb[:], kq_params).then_inc(kq_in, 16)

            def copy_ct(h):
                act.wait_ge(cT_ps, h + 1)
                act.activation(cT[:, h * W:(h + 1) * W], ps[4 * h][:], ACT.Copy).then_inc(cT_done, 1)

            def elu_parts(h, ready, bank, exp, relu, bias, done):
                s = slice(h * W, (h + 1) * W)
                act.wait_ge(ready, h + 1)
                act.activation(exp[:, s], bank[:], ACT.Exp, bias=bias).then_inc(done, 1)
                act.activation(relu[:, s], bank[:], ACT.Relu, bias=bias).then_inc(done, 1)

            def copy_xnt(h):
                act.wait_ge(xnT_ps, h + 1)
                act.activation(xnT[:, h * W:(h + 1) * W], ps[4 * h + 1][:], ACT.Copy).then_inc(xnT_done, 1)

            def value(h):
                act.wait_ge(v_ps, h + 1)
                act.activation(v[:, h * W:(h + 1) * W], ps[4 * h + 1][:], ACT.Identity, bias=bv_sb).then_inc(v_done, 1)

            act.wait_ge(kq_in, 16)
            act.activation(tg[:], g_sb, ACT.Tanh).then_inc(tg_done, 1)
            copy_ct(0)
            elu_parts(0, k_ps, ps[2], kexp, krelu, bk_sb, k_act)
            copy_ct(1)
            act.wait_ge(vcr_in, 16)
            value(0)
            elu_parts(1, k_ps, ps[6], kexp, krelu, bk_sb, k_act)
            act.wait_ge(wrc_ps, 1)
            act.activation(wr_centred[:], ps[7][:, 0:E], ACT.Copy).then_inc(wrc_done, 1)
            copy_xnt(0)
            value(1)
            copy_xnt(1)
            elu_parts(0, q_ps, ps[3], qexp, qrelu, bq_sb, q_act)
            elu_parts(1, q_ps, ps[7], qexp, qrelu, bq_sb, q_act)

            def copy_x1t(h):
                act.wait_ge(x1T_ps, h + 1)
                act.activation(x1T[:, h * W:(h + 1) * W], ps[4 * h + 3][:], ACT.Copy).then_inc(x1T_done, 1)

            def exp_below(h):
                ts = slice(h * TH, (h + 1) * TH)
                act.wait_ge(scaled_done, h + 1)
                act.activation(expo[:, ts, :], below_scaled[:, ts, :], ACT.Exp).then_inc(expo_done, 1)

            def normalise2(h):
                act.wait_ge(minus_mu_done, h + 1)
                for t in range(h * TH, (h + 1) * TH):
                    act.activation(xn2[:, t, :], rows[:, t, 0:D], ACT.Identity, bias=minus_mu[:, t:t + 1],
                                   scale=rows[:, t, RS:RS + 1]).then_inc(xn2_done, 1)

            copy_x1t(0)
            copy_x1t(1)
            exp_below(0)
            normalise2(0)
            exp_below(1)
            normalise2(1)
            act.wait_ge(expo_done, NH)
            act.activation(gelu_warm[:], expo[:, 0, 0:1], ACT.Gelu)
            act.wait_ge(eb_done, 1)
            for b in range(RING, RING + EARLY):
                load_w1(act, b, w1_sb[:, b - RING, :], w1_in[b - RING], None)

            def copy_sxt(p):
                a, z = PACKS[p]
                act.wait_ge(sxT_ps, p + 1)
                act.activation(sxT[:, a:z, :],
                               ps[6 + p % 2][:, 0:(z - a) * P].rearrange("p (b s) -> p b s", s=P),
                               ACT.Copy).then_inc(sxT_done, 1)

            def gelu(b, u, e, read):
                if read is not None:
                    act.wait_ge(e_ps, read)
                act.wait_ge(h_ps, b + 1)
                for c in range(FC):
                    last = act.activation(hid[:, u, c, :], ps[u][:, c * P:(c + 1) * P], ACT.Gelu,
                                          bias=b1_sb[:, bass.ds(e, 1), c])
                last.then_inc(hid_done, 1)

            act.wait_ge(start_done, 1)
            firsts = [first_slot_of(act, b) for b in BY_SCALAR]
            early_experts = [expert_of(act, b) for b in range(EARLY)]
            e = expert_of(act, EARLY)
            for b in range(EARLY):
                copy_sxt(b)
            for b in range(EARLY):
                gelu(b, b, early_experts[b], None)
            copy_sxt(2)
            copy_sxt(3)
            act.wait_ge(slots_written, 16 * NT)
            for b, first in zip(BY_SCALAR, firsts):
                load_rows(act, b, first)
            copy_sxt(4)
            for b in range(EARLY, 2 * RING):
                gelu(b, b % RING, e, b - (RING - 1) if b >= RING else None)
                if b < 2 * RING - 1:
                    e = expert_of(act, b + 1)
                if b > EARLY:
                    copy_sxt(b + 2)
            copy_sxt(2 * RING + 2)
            with act.Fori(2, G) as i:
                for u in range(RING):
                    gelu(RING * i + u, u, expert_of(act, RING * i + u), RING * i + u - (RING - 1))

        @block.vector
        def _(dve):
            dve.memset(ones[:], 1.0).then_inc(ones_made, 1)
            dve.wait_ge(diff_made, 1)
            dve.tensor_scalar(ident[:], diff[:], float(P), None, ALU.is_equal).then_inc(ident_made, 1)
            dve.tensor_copy(diff_i[:], diff[:]).then_inc(depth_made, 1)
            dve.tensor_scalar(before[:], diff[:], float(P), None, ALU.is_gt).then_inc(masks_made, 1)
            dve.wait_ge(depth_made, 1)
            dve.tensor_scalar(depth_diff[:], diff_i[:], D // HEADS - 1, None, ALU.bitwise_and).then_inc(depth_made, 1)
            dve.wait_ge(depth_made, 2)
            dve.tensor_scalar(same_depth[:], depth_diff[:], 0.0, None, ALU.is_equal).then_inc(depth_made, 1)
            dve.wait_ge(depth_made, 3)
            dve.scalar_tensor_tensor(head_sum[:], diff[:], float(P), same_depth[:], ALU.is_ge, ALU.mult)\
                .then_inc(masks_made, 1)
            dve.wait_ge(ident_made, 1)
            dve.tensor_scalar(centre[:], ident[:], 1.0 / D, None, ALU.subtract).then_inc(centre_made, 1)

            def moments(src, to, t, done):
                dve.bn_stats(to[:, t, :], src[:, t, 0:D]).then_inc(done, 1)

            def half_moments(h, src, to, arrived, count, done):
                dve.wait_ge(arrived, count)
                for t in range(h * TH, (h + 1) * TH):
                    moments(src, to, t, done)

            def mean_var(h, moments_of, pair, moments_done, done):
                for t in range(h * TH, (h + 1) * TH):
                    dve.wait_ge(moments_done, t + 1)
                    dve.bn_aggr(pair[:, t, :], moments_of[:, t, :]).then_inc(done, 1)

            for h in range(NH):
                half_moments(h, x_sb, stats, x_in[h], 16, st_done)
                mean_var(h, stats, mv, st_done, mv_done)

            def normalise(h):
                dve.wait_ge(rstd_done, h + 1)
                for t in range(h * TH, (h + 1) * TH):
                    last = dve.tensor_scalar(xn[:, t, :], x_sb[:, t, :], mv[:, t, 0:1], mv[:, t, 1:2],
                                             ALU.subtract, ALU.mult)
                last.then_inc(xn_done, 1)

            def elu_sum(dst, exp, relu, h, arrived, done):
                s = slice(h * W, (h + 1) * W)
                dve.wait_ge(arrived, 2 * h + 2)
                dve.scalar_tensor_tensor(dst[:, s], exp[:, s], 1.0, relu[:, s], ALU.min, ALU.add).then_inc(done, 1)

            def inverse(h):
                dve.wait_ge(sum_ps, h + 1)
                dve.reciprocal(inv[:, h * W:(h + 1) * W], ps[4 * h][:]).then_inc(inv_done, 1)

            elu_sum(kf, kexp, krelu, 0, k_act, kf_done)
            normalise(0)
            normalise(1)
            elu_sum(kf, kexp, krelu, 1, k_act, kf_done)
            inverse(0)
            elu_sum(qf, qexp, qrelu, 0, q_act, qf0_done)
            inverse(1)

            def attend(h, ready):
                s = slice(h * W, (h + 1) * W)
                dve.wait_ge(inv_done, h + 1)
                dve.wait_ge(ready, 1)
                dve.tensor_tensor(attn[:, s], vqk[:, s], inv[:, s], ALU.mult).then_inc(attn_done, 1)

            attend(0, vqk0_done)
            s = slice(W, T)
            elu_sum(qf, qexp, qrelu, 1, q_act, qf1_done)
            dve.wait_ge(qf1_done, 1)
            dve.wait_ge(vk_done, NH)
            dve.tensor_tensor(vqk[:, s], vk[:, s], qf[:, s], ALU.mult).then_inc(vqk1_done, 1)
            dve.wait_ge(iotas_made, 4)
            dve.tensor_scalar(not_later[:], ediff[:], 0.0, None, ALU.is_ge).then_inc(not_later_made, 1)

            def add_attention(h):
                ts = slice(h * TH, (h + 1) * TH)
                dve.wait_ge(y_ps, h + 1)
                dve.wait_ge(xb_done, h + 1)
                dve.scalar_tensor_tensor(rows[:, ts, 0:D], ps[4 * h + 2][:].rearrange("p (t d) -> p t d", d=D), tg[:, 0:1],
                                         xb[:, ts, :], ALU.mult, ALU.add).then_inc(x1_done, 1)

            pair2 = rows[:, :, MU:MU + 2]

            te = [P, TH, E]

            def choose(h, meanwhile):
                ts = slice(h * TH, (h + 1) * TH)
                logit = ps[4 * h][:, 0:TH * E].rearrange("p (t e) -> p t e", e=E)

                def other_tile(j):
                    if meanwhile is not None:
                        moments(rows, stats2, meanwhile * TH + j, st2_done)

                if meanwhile is not None:
                    dve.wait_ge(x1_done, meanwhile + 1)
                dve.wait_ge(logit_ps, h + 1)
                dve.reduce_max(top[:, ts], logit, AX_X).then_inc(top_done, 1)
                other_tile(0)
                dve.wait_ge(top_done, h + 1)
                dve.tensor_tensor(hit[:, ts, :], logit, top[:, ts].unsqueeze(2).broadcast_to(te),
                                  ALU.is_equal).then_inc(hit_done, 1)
                dve.tensor_tensor(below[:, ts, :], logit, top[:, ts].unsqueeze(2).broadcast_to(te),
                                  ALU.subtract).then_inc(below_done, 1)
                other_tile(1)
                dve.wait_ge(hit_done, h + 1)
                dve.tensor_tensor(score[:, ts, :], hit[:, ts, :], rev[:].unsqueeze(1).broadcast_to(te),
                                  ALU.mult).then_inc(score_done, 1)
                other_tile(2)
                dve.wait_ge(score_done, h + 1)
                dve.reduce_max(best[:, ts], score[:, ts, :], AX_X).then_inc(best_done, 1)
                other_tile(3)
                dve.wait_ge(best_done, h + 1)
                dve.tensor_tensor(onehot[:, ts, :], score[:, ts, :], best[:, ts].unsqueeze(2).broadcast_to(te),
                                  ALU.is_equal).then_inc(onehot_done, 1)

            def scale_below(h):
                ts = slice(h * TH, (h + 1) * TH)
                dve.wait_ge(below_done, h + 1)
                dve.wait_ge(rstd2_done, h + 1)
                dve.tensor_tensor(below_scaled[:, ts, :], below[:, ts, :],
                                  rows[:, ts, RS:RS + 1].broadcast_to(te), ALU.mult).then_inc(scaled_done, 1)
                dve.scalar_tensor_tensor(minus_mu[:, ts], rows[:, ts, MU], -1.0, rows[:, ts, RS], ALU.mult,
                                         ALU.mult).then_inc(minus_mu_done, 1)

            def sum_exps(h):
                dve.wait_ge(expo_done, h + 1)
                dve.reduce_sum(total[:, h * TH:(h + 1) * TH], expo[:, h * TH:(h + 1) * TH, :], AX_X)\
                    .then_inc(total_done, 1)

            def invert_sum(h):
                dve.wait_ge(total_done, h + 1)
                dve.reciprocal(pmax[:, h * TH:(h + 1) * TH], total[:, h * TH:(h + 1) * TH]).then_inc(pmax_done, 1)

            def gate(h):
                ts = slice(h * TH, (h + 1) * TH)
                dve.wait_ge(pmax_done, h + 1)
                dve.tensor_scalar(rows[:, ts, GATE], pmax[:, ts], tg[:, 1:2], None, ALU.mult).then_inc(gate_done, 1)

            def place(h):
                ts = slice(h * TH, (h + 1) * TH)
                rank = ps[4 * h + 1][:, 0:TH * E].rearrange("p (t e) -> p t e", e=E)
                dve.wait_ge(rank_ps, h + 1)
                dve.tensor_tensor(placed[:, ts, :], rank, onehot[:, ts, :], ALU.mult).then_inc(placed_done, 1)

            def slot(h):
                dve.wait_ge(placed_done, h + 1)
                dve.reduce_sum(pos_f[:, h * TH:(h + 1) * TH], placed[:, h * TH:(h + 1) * TH, :], AX_X)\
                    .then_inc(posf_done, 1)

            def slot_as_int(h):
                dve.wait_ge(posf_done, h + 1)
                dve.tensor_copy(pos[:, h * TH:(h + 1) * TH], pos_f[:, h * TH:(h + 1) * TH]).then_inc(pos_done, 1)

            add_attention(0)
            attend(1, vqk1_done)
            half_moments(0, rows, stats2, x1_done, 1, st2_done)
            mean_var(0, stats2, pair2, st2_done, mv2_done)
            add_attention(1)
            choose(0, 1)
            mean_var(1, stats2, pair2, st2_done, mv2_done)
            scale_below(0)
            place(0)
            sum_exps(0)
            slot(0)
            invert_sum(0)
            slot_as_int(0)
            gate(0)
            choose(1, None)
            scale_below(1)
            dve.wait_ge(count_ps, 1)
            dve.tensor_scalar(padded[:], ps[0][:, 0:E], float(P - 1), None, ALU.add).then_inc(padded_done, 1)
            place(1)
            dve.wait_ge(padded_done, 1)
            dve.tensor_scalar(room[:], padded[:], 7, 7, ALU.logical_shift_right, ALU.logical_shift_left)\
                .then_inc(room_done, 1)
            sum_exps(1)
            dve.wait_ge(room_done, 1)
            dve.wait_ge(not_later_made, 1)
            dve.tensor_tensor(eprod[:], not_later[:], room[:].unsqueeze(1).broadcast_to([P, E, E]), ALU.mult)\
                .then_inc(eprod_done, 1)
            slot(1)
            dve.wait_ge(eprod_done, 1)
            dve.reduce_sum(stop_of[:], eprod[:], AX_X).then_inc(stop_done, 1)
            invert_sum(1)
            be = [P, BLOCKS, E]
            dve.wait_ge(stop_done, 1)
            dve.tensor_tensor(passed[:], stop_of[:].unsqueeze(1).broadcast_to(be),
                              first_slot[:].unsqueeze(2).broadcast_to(be), ALU.is_le).then_inc(passed_done, 1)
            slot_as_int(1)
            dve.wait_ge(passed_done, 1)
            dve.reduce_sum(eb_f[:], passed[:], AX_X).then_inc(ebf_done, 1)
            gate(1)
            dve.wait_ge(ebf_done, 1)
            dve.tensor_scalar(eb[:], eb_f[0:1, :], float(E - 1), None, ALU.min).then_inc(eb_done, 1)
            dve.tensor_tensor(room_before[:], passed[:], room[:].unsqueeze(1).broadcast_to(be),
                              ALU.mult).then_inc(room_before_done, 1)
            dve.scalar_tensor_tensor(slot_sum[:], eb_f[:], float(T), first_slot[:], ALU.mult, ALU.add)\
                .then_inc(slot_sum_done, 1)
            dve.wait_ge(room_before_done, 1)
            dve.reduce_sum(used_before[:], room_before[:], AX_X).then_inc(used_done, 1)
            dve.wait_ge(used_done, 1)
            dve.wait_ge(slot_sum_done, 1)
            dve.tensor_tensor(start_f[:], slot_sum[:], used_before[:], ALU.subtract).then_inc(startf_done, 1)
            dve.wait_ge(startf_done, 1)
            dve.tensor_scalar(start[:], start_f[0:1, :], float(NONE), None, ALU.min).then_inc(start_done, 1)
            for b in range(EARLY):
                dve.tensor_scalar(slot_in[:, b, :], pos_f[:], start_f[:, b:b + 1], None, ALU.subtract)\
                    .then_inc(slot_in_done, 1)
            dve.wait_ge(slot_in_done, EARLY)
            for b in range(EARLY):
                for t in range(NT):
                    dve.tensor_scalar(select[:, b, t, :], slot_no[:], slot_in[:, b, t:t + 1], None,
                                      ALU.is_equal).then_inc(select_done, 1)

            def normalise_slots(p):
                a, z = PACKS[p]
                dve.wait_ge(rows_in[p], 16 * (z - a))
                for b in range(a, z):
                    last = dve.tensor_scalar(sx[:, b, :], slot_rows[:, b, 0:D], slot_rows[:, b, MU:MU + 1],
                                             slot_rows[:, b, RS:RS + 1], ALU.subtract, ALU.mult)
                last.then_inc(sx_done, 1)

            def add_bias(b, e):
                dve.scalar_tensor_tensor(xb2[:, bass.ds(b, 1), :].rearrange("p o d -> p (o d)"),
                                         b2_sb[:, bass.ds(e, 1), :].rearrange("p o d -> p (o d)"),
                                         slot_rows[:, bass.ds(b, 1), GATE],
                                         slot_rows[:, bass.ds(b, 1), 0:D].rearrange("p o d -> p (o d)"),
                                         ALU.mult, ALU.add).then_inc(xb2_done, 1)

            def residual(b, u):
                dve.wait_ge(xb2_done, b + 1)
                dve.wait_ge(e_ps, b + 1)
                dve.scalar_tensor_tensor(res[:, bass.ds(b, 1), :].rearrange("p o d -> p (o d)"), ps[3 + u][:, 0:D],
                                         slot_rows[:, bass.ds(b, 1), GATE],
                                         xb2[:, bass.ds(b, 1), :].rearrange("p o d -> p (o d)"),
                                         ALU.mult, ALU.add).then_inc(res_done, 1)

            dve.wait_ge(b2_in, 16)
            dve.wait_ge(eb_done, 1)
            early_experts = [expert_of(dve, b) for b in range(EARLY)]
            for p in range(EARLY, 5):
                normalise_slots(p)
            for b in range(EARLY):
                dve.wait_ge(rows_in[b], 16)
                add_bias(b, early_experts[b])
                residual(b, b)
            normalise_slots(5)
            add_bias(EARLY, expert_of(dve, EARLY))
            add_bias(EARLY + 1, expert_of(dve, EARLY + 1))
            for b in range(EARLY, 2 * RING):
                e = expert_of(dve, b + 2)
                if b == 2 * RING - 2:
                    normalise_slots(b + 4)
                add_bias(b + 2, e)
                residual(b, b % RING)
                if b < 2 * RING - 2:
                    normalise_slots(b + 4)
            with dve.Fori(2, G - 1) as i:
                for u in range(RING):
                    b = RING * i + u
                    add_bias(b + 2, expert_of(dve, b + 2))
                    residual(b, u)
            for b in range(BLOCKS - RING, BLOCKS):
                if b + 2 < BLOCKS:
                    add_bias(b + 2, expert_of(dve, b + 2))
                residual(b, b % RING)

        @block.tensor
        def _(pe):
            def turn(dst, src):
                return pe.transpose(dst, src, ident[:])

            def keep_warm(products, bank):
                for _ in range(products):
                    pe.matmul(ps[bank][:].rearrange("p (t s) -> p t s", s=P), ones[:],
                              ones[:].unsqueeze(1).broadcast_to([P, TH, P]), start=True, stop=True)

            pe.wait_ge(ones_made, 1)
            keep_warm(WARM_START, 7)
            pe.wait_ge(ident_made, 1)

            def turn_c(h):
                pe.wait_ge(c_in[h], 16)
                for t in range(TH):
                    mm = turn(ps[4 * h][:, t * P:(t + 1) * P], c_sb[:, h * TH + t, :])
                mm.then_inc(cT_ps, 1)

            def turn_xn(h):
                pe.wait_ge(v_done, h + 1)
                pe.wait_ge(xn_done, h + 1)
                for t in range(TH):
                    mm = turn(ps[4 * h + 1][:, t * P:(t + 1) * P], xn[:, h * TH + t, :])
                mm.then_inc(xnT_ps, 1)

            def keys(h):
                pe.wait_ge(cT_done, h + 1)
                pe.matmul(ps[4 * h + 2][:], wk_sb, cT[:, h * W:(h + 1) * W], start=True, stop=True).then_inc(k_ps, 1)

            def queries(h):
                pe.wait_ge(xnT_done, h + 1)
                pe.matmul(ps[4 * h + 3][:], wq_sb, xnT[:, h * W:(h + 1) * W], start=True, stop=True).then_inc(q_ps, 1)

            def sums(h):
                pe.wait_ge(kf_done, h + 1)
                pe.matmul(ps[4 * h][:], head_sum[:], kf[:, h * W:(h + 1) * W], start=True, stop=True).then_inc(sum_ps, 1)

            def values(h):
                pe.matmul(ps[4 * h + 1][:], wv_sb, cT[:, h * W:(h + 1) * W], start=True, stop=True).then_inc(v_ps, 1)

            turn_c(0)
            keep_warm(2, 7)
            pe.wait_ge(kq_in, 16)
            keys(0)
            turn_c(1)
            keep_warm(1, 7)
            pe.wait_ge(vcr_in, 16)
            values(0)
            pe.wait_ge(centre_made, 1)
            pe.matmul(ps[7][:, 0:E], centre[:], wr_sb, start=True, stop=True).then_inc(wrc_ps, 1)
            keys(1)
            pe.wait_ge(masks_made, 2)
            sums(0)
            turn_xn(0)
            values(1)
            queries(0)
            turn_xn(1)
            sums(1)
            pe.wait_ge(wrc_done, 1)
            queries(1)
            pe.wait_ge(q_act, 2 * NH)
            keep_warm(WARM, 7)
            pe.wait_ge(inv_done, NH)
            keep_warm(2, 7)

            def attended(h):
                pe.wait_ge(attn_done, h + 1)
                for t in range(TH):
                    mm = pe.matmul(ps[4 * h + 2][:, t * P:(t + 1) * P], attn[:, (h * TH + t) * P:(h * TH + t + 1) * P],
                                   wc_sb, start=True, stop=True)
                mm.then_inc(y_ps, 1)

            def turn_x1(h):
                pe.wait_ge(x1_done, h + 1)
                for t in range(TH):
                    mm = turn(ps[4 * h + 3][:, t * P:(t + 1) * P], rows[:, h * TH + t, 0:D])
                mm.then_inc(x1T_ps, 1)

            def logits(h):
                pe.wait_ge(x1T_done, h + 1)
                for t in range(TH):
                    mm = pe.matmul(ps[4 * h][:, t * E:(t + 1) * E], x1T[:, (h * TH + t) * P:(h * TH + t + 1) * P],
                                   wr_centred[:], start=True, stop=True)
                mm.then_inc(logit_ps, 1)

            def ranks(h):
                R = ps[4 * h + 1]
                a, z = h * TH, (h + 1) * TH
                pe.wait_ge(onehot_done, h + 1)
                pe.matmul(R[:, 0:TH * E], ones[0:1, :], expert_slot[:].rearrange("o t e -> o (t e)"), start=True, stop=False)
                for t in range(z - 1):
                    to = max(t + 1 - a, 0)
                    pe.matmul(R[:, to * E:TH * E].rearrange("p (t e) -> p t e", e=E), ones[:],
                              onehot[:, t:t + 1, :].broadcast_to([P, TH - to, E]),
                              start=False, stop=False, skip_group_check=True)
                pe.matmul(R[:, 0:TH * E], before[:], onehot[:, a:z, :].rearrange("p t e -> p (t e)"),
                          start=False, stop=True).then_inc(rank_ps, 1)

            attended(0)
            keep_warm(2, 7)
            turn_x1(0)
            attended(1)
            logits(0)
            turn_x1(1)
            keep_warm(2, 3)
            pe.wait_ge(eslot_made, 1)
            ranks(0)
            logits(1)
            pe.wait_ge(onehot_done, NH)
            for t in range(NT):
                mm = pe.matmul(ps[0][:, 0:E], ones[:], onehot[:, t, :], start=(t == 0), stop=(t == NT - 1))
            mm.then_inc(count_ps, 1)
            ranks(1)
            keep_warm(2 * WARM, 3)

            def gather(b):
                for t in range(NT):
                    pe.wait_ge(xn2_done, t + 1)
                    pe.wait_ge(select_done, NT * b + t + 1)
                    mm = pe.matmul(ps[6 + b][:, 0:P], xn2[:, t, :], select[:, b, t, :],
                                   start=(t == 0), stop=(t == NT - 1))
                mm.then_inc(sxT_ps, 1)

            def turn_sx(p):
                a, z = PACKS[p]
                pe.wait_ge(sx_done, p - EARLY + 1)
                if p >= 2:
                    pe.wait_ge(sxT_done, p - 1)
                for b in range(a, z):
                    mm = turn(ps[6 + p % 2][:, (b - a) * P:(b - a + 1) * P], sx[:, b, :])
                mm.then_inc(sxT_ps, 1)

            def hidden(b, u, nth):
                weights = w1_early if nth is None else w1_sb
                if nth is None:
                    pe.wait_ge(w1_early_in[u], 16)
                else:
                    pe.wait_ge(w1_in[u], 16 * nth)
                for c in range(FC):
                    mm = pe.matmul(ps[u][:, c * P:(c + 1) * P], weights[:, u, c * P:(c + 1) * P],
                                   sxT[:, bass.ds(b, 1), :].rearrange("p o s -> p (o s)"),
                                   start=True, stop=True)
                mm.then_inc(h_ps, 1)

            def result(b, u, e, read):
                to = ps[3 + u][:, 0:D]
                if read is not None:
                    pe.wait_ge(res_done, read)
                pe.wait_ge(hid_done, b + 1)
                for c in range(FC):
                    mm = pe.matmul(to, hid[:, u, c, :], w2_sb[c][:, bass.ds(e, 1), :].rearrange("p o d -> p (o d)"),
                                   start=(c == 0), stop=(c == FC - 1))
                mm.then_inc(e_ps, 1)

            pe.wait_ge(eb_done, 1)
            pe.wait_ge(w2_in, 16 * FC)
            gather(0)
            gather(1)
            pe.wait_ge(sxT_done, 1)
            hidden(0, 0, None)
            pe.wait_ge(sxT_done, 2)
            hidden(1, 1, None)
            for b in range(EARLY):
                result(b, b, expert_of(pe, b), None)
            turn_sx(2)
            turn_sx(3)
            pe.wait_ge(sxT_done, 3)
            hidden(2, 2, 1)
            turn_sx(4)
            pe.wait_ge(sxT_done, 4)
            hidden(3, 0, 1)
            for b in range(EARLY, 2 * RING):
                e = expert_of(pe, b)
                if b == 2 * RING - 1:
                    turn_sx(b + 3)
                pe.wait_ge(sxT_done, pack_of(b + 2) + 1)
                hidden(b + 2, (b + 2) % RING, b // RING + 1)
                result(b, b % RING, e, b - (RING - 1) if b >= RING else None)
                if b < 2 * RING - 1:
                    turn_sx(b + 3)
            pe.wait_ge(sxT_done, len(PACKS))
            with pe.Fori(2, G - 1) as i:
                for u in range(RING):
                    b = RING * i + u
                    e = expert_of(pe, b)
                    hidden(b + 2, (u + 2) % RING, i + 1)
                    result(b, u, e, b - (RING - 1))
            for b in range(BLOCKS - RING, BLOCKS):
                e = expert_of(pe, b)
                if b + 2 < BLOCKS:
                    hidden(b + 2, (b + 2) % RING, G)
                result(b, b % RING, e, b - (RING - 1))


_OUTS = [((8, 128, 128), 'float32')]


def kernel(**inputs):
    import numpy as _np
    import concourse.bacc as _bacc
    from concourse import mybir as _mybir
    from concourse.bass_utils import run_bass_kernel_spmd as _run

    a = {name: _np.asarray(value) for name, value in inputs.items()}
    P = 128

    def rows(v):
        return _np.broadcast_to(v, (P, v.shape[-1]))

    def column(v):
        return v.reshape(P, 1)

    laid = {
        'x': a['x'],
        'ctx': a['ctx_1024'],
        'kq_params': _np.concatenate([a['L0_xattn_wk_w'], a['L0_xattn_wq_w'], column(a['L0_xattn_wk_b']),
                                      column(a['L0_xattn_wq_b']), rows(a['g_xattn']), rows(a['g_ffn'])], axis=1),
        'vcr_params': _np.concatenate([a['L0_xattn_wv_w'], a['L0_xattn_wc_w'], a['L0_ffn_Wr'],
                                       column(a['L0_xattn_wv_b']), rows(a['L0_xattn_wc_b']),
                                       a['L0_ffn_b1'].reshape(-1, P).T], axis=1),
        'w1': a['L0_ffn_W1'],
        'w2': a['L0_ffn_W2'],
        'b2': a['L0_ffn_b2'],
    }
    nc = _bacc.Bacc("TRN2", target_bir_lowering=False, num_devices=1)
    arrays, args = {}, []
    for name, value in laid.items():
        value = _np.ascontiguousarray(value)
        arrays[f"in_{name}_dram"] = value
        args.append(nc.dram_tensor(f"in_{name}_dram", value.shape, _mybir.dt.from_np(value.dtype),
                                   kind="ExternalInput").ap())
    for i, (shape, dtype) in enumerate(_OUTS):
        dt = _mybir.dt.from_np(_np.dtype(dtype))
        args.append(nc.dram_tensor(f"out_{i}_dram", shape, dt, kind="ExternalOutput").ap())
    gated_block_kernel(nc, *args)
    r = _run(nc, [arrays], core_ids=[0])
    return r.results[0]["out_0_dram"]
```
